# Optimizing a Trainium2 kernel written in Bass

```python
import numpy as np
import jax
import jax.numpy as jnp

def _softmax(x, axis=-1):
    return jax.nn.softmax(x, axis=axis)

def _gelu(x):
    return jax.nn.gelu(x, approximate=True)

def _silu(x):
    return jax.nn.silu(x)

def _sigmoid(x):
    return jax.nn.sigmoid(x)

def _layernorm(x, axis=-1, eps=1e-05):
    m = jnp.mean(x, axis=axis, keepdims=True)
    v = jnp.var(x, axis=axis, keepdims=True)
    return (x - m) / jnp.sqrt(v + eps)

def _scatter_add(tgt, idx, src, axis=0):
    return tgt.at[idx].add(src)

def _segment_sum(src, seg, n):
    return jax.ops.segment_sum(src, seg, n)
kernel_name = 'mk_macaron_d1_jaxref_r8_c54fbb'

def setup_inputs(seed: int=0):
    np.random.seed(seed)
    _w = jnp.asarray

    def _L0_attn_setup():
        import jax, jax.numpy as jnp
        import numpy as np
        key = jax.random.key(seed)
        ks = jax.random.split(key, 5)
        B, T, D = (4, 512, 128)
        x = jax.random.normal(ks[0], (B, T, D), dtype=jnp.float32)
        Wqkv = jax.random.normal(ks[1], (D, 3 * D), dtype=jnp.float32) * D ** (-0.5)
        bqkv = jax.random.normal(ks[2], (3 * D,), dtype=jnp.float32) * 0.02
        Wout = jax.random.normal(ks[3], (D, D), dtype=jnp.float32) * D ** (-0.5)
        bout = jax.random.normal(ks[4], (D,), dtype=jnp.float32) * 0.02
        return {'x': x, 'Wqkv': Wqkv, 'bqkv': bqkv, 'Wout': Wout, 'bout': bout}
    _L0_attn_in = _L0_attn_setup()

    def _L0_ffn_setup():
        import jax, jax.numpy as jnp
        import numpy as np
        N_EMBD = 128
        NUM_EXPERTS = 8
        TOP_K = 2
        D_FF = 4 * N_EMBD
        B, S = (4, 256)
        key = jax.random.key(seed)
        ks = jax.random.split(key, 7)
        scale = lambda fan_in: 1.0 / np.sqrt(fan_in)
        x = jax.random.normal(ks[0], (B, S, N_EMBD), dtype=jnp.float32)
        W_router = jax.random.normal(ks[1], (N_EMBD, NUM_EXPERTS), dtype=jnp.float32) * scale(N_EMBD)
        b_router = jnp.zeros((NUM_EXPERTS,), dtype=jnp.float32)
        W1 = jax.random.normal(ks[2], (NUM_EXPERTS, N_EMBD, D_FF), dtype=jnp.float32) * scale(N_EMBD)
        b1 = jnp.zeros((NUM_EXPERTS, D_FF), dtype=jnp.float32)
        W2 = jax.random.normal(ks[3], (NUM_EXPERTS, D_FF, N_EMBD), dtype=jnp.float32) * scale(D_FF)
        b2 = jnpp = jnp.zeros((NUM_EXPERTS, N_EMBD), dtype=jnp.float32)
        return {'x': x, 'W_router': W_router, 'b_router': b_router, 'W1': W1, 'b1': b1, 'W2': W2, 'b2': b2}
    _L0_ffn_in = _L0_ffn_setup()
    _d = {'L0_attn_x': _L0_attn_in['x'], 'L0_attn_Wqkv': _L0_attn_in['Wqkv'], 'L0_attn_bqkv': _L0_attn_in['bqkv'], 'L0_attn_Wout': _L0_attn_in['Wout'], 'L0_attn_bout': _L0_attn_in['bout'], 'L0_ffn_W_router': _L0_ffn_in['W_router'], 'L0_ffn_b_router': _L0_ffn_in['b_router'], 'L0_ffn_W1': _L0_ffn_in['W1'], 'L0_ffn_b1': _L0_ffn_in['b1'], 'L0_ffn_W2': _L0_ffn_in['W2'], 'L0_ffn_b2': _L0_ffn_in['b2']}
    _x0 = _d['L0_attn_x']
    _d['L0_attn_x'] = jax.random.normal(jax.random.fold_in(jax.random.key(seed), 1), (4, 512, 128), dtype=_x0.dtype)
    del _x0
    return _d

def reference(L0_attn_x, L0_attn_Wqkv, L0_attn_bqkv, L0_attn_Wout, L0_attn_bout, L0_ffn_W_router, L0_ffn_b_router, L0_ffn_W1, L0_ffn_b1, L0_ffn_W2, L0_ffn_b2):

    def _L0_attn_ref(x, Wqkv, bqkv, Wout, bout):
        import jax, jax.numpy as jnp
        import numpy as np
        qkv = jnp.einsum('btd,de->bte', x, Wqkv) + bqkv
        q, k, v = jnp.split(qkv, 3, axis=-1)
        q = q / jnp.linalg.norm(q, axis=-1, keepdims=True)
        k = k / jnp.linalg.norm(k, axis=-1, keepdims=True)
        kv = jnp.sum(k * v, axis=-2, keepdims=True)
        out = q * kv
        return jnp.einsum('btd,de->bte', out, Wout) + bout

    def _L0_ffn_ref(x, W_router, b_router, W1, b1, W2, b2):
        import jax, jax.numpy as jnp
        import numpy as np
        N_EMBD = 128
        NUM_EXPERTS = 8
        TOP_K = 2
        D_FF = 4 * N_EMBD
        B, S = (4, 256)
        Bv, Sv, D = x.shape
        flat_x = x.reshape(-1, D)
        T = flat_x.shape[0]
        logits = flat_x @ W_router + b_router
        top_vals, top_idx = jax.lax.top_k(logits, TOP_K)
        neg_inf = jnp.full_like(logits, -jnp.inf)
        sparse_logits = neg_inf.at[jnp.arange(T)[:, None], top_idx].set(top_vals)
        router_weights = jax.nn.softmax(sparse_logits, axis=-1)
        final_output = jnp.zeros_like(flat_x)
        for e in range(NUM_EXPERTS):
            expert_mask = jnp.any(top_idx == e, axis=-1)
            h = jax.nn.relu(flat_x @ W1[e] + b1[e])
            y = h @ W2[e] + b2[e]
            w = router_weights[:, e] * expert_mask.astype(x.dtype)
            final_output = final_output + y * w[:, None]
        return final_output.reshape(Bv, Sv, D)
    x = L0_attn_x
    x = x + 0.5 * _L0_ffn_ref(_layernorm(x, axis=-1), L0_ffn_W_router, L0_ffn_b_router, L0_ffn_W1, L0_ffn_b1, L0_ffn_W2, L0_ffn_b2)
    x = x + _L0_attn_ref(_layernorm(x, axis=-1), L0_attn_Wqkv, L0_attn_bqkv, L0_attn_Wout, L0_attn_bout)
    x = x + 0.5 * _L0_ffn_ref(_layernorm(x, axis=-1), L0_ffn_W_router, L0_ffn_b_router, L0_ffn_W1, L0_ffn_b1, L0_ffn_W2, L0_ffn_b2)
    return x

_drawn_inputs = setup_inputs


def setup_inputs(seed=0):
    import zlib

    import numpy as np

    out = dict(_drawn_inputs(seed))
    spreads = {'L0_ffn_b_router': (0.0, 0.1), 'L0_ffn_b1': (0.0, 0.1), 'L0_ffn_b2': (0.0, 0.1)}
    factors = {'L0_attn_bqkv': 2.812}
    for name, (base, spread) in spreads.items():
        noise = np.random.default_rng([zlib.crc32(name.encode()), seed]).standard_normal(out[name].shape)
        drawn = base * np.exp(spread * noise) if base else spread * noise
        out[name] = jnp.asarray(drawn.astype(out[name].dtype))
    for name, factor in factors.items():
        out[name] = (out[name] * factor).astype(out[name].dtype)
    return out
```

```python
from contextlib import ExitStack

import concourse.bass as bass
from concourse import mybir

P = 128
F32 = mybir.dt.float32
F16 = mybir.dt.float16
I32 = mybir.dt.int32
ALU = mybir.AluOpType
ACT = mybir.ActivationFunctionType
AX_X = mybir.AxisListType.X
EPS = 1e-5
W_SCALE = 64.0
FAR = -3.0e38


def macaron(nc, x, w_qkv, b_qkv, w_out, b_out, w_router, b_router, w1, b1, w2, b2, out):
    BATCH, SEQ, D = x.shape
    E, _, FF = w1.shape
    CH = FF // P
    TB = SEQ // P
    NB = 2
    LAYERS = 2
    BB = BATCH // NB
    NT = BB * TB
    BLOCK = NT * P
    SLOT_TILES = (2 * BLOCK + E * (P - 1)) // P
    GROUP = TB * D
    NG, NY = 4, 4
    assert D == P and BATCH % NB == 0

    x_v = x.rearrange("b (p j) d -> b p j d", j=TB)
    out_v = out.rearrange("b (p j) d -> b p j d", j=TB)
    tok_rows = [nc.dram_tensor(f"tok_rows{k}", (BLOCK, 2 * D), F16, kind="Internal").ap() for k in range(NB)]
    slot_rows = [nc.dram_tensor(f"slot_rows{k}", (SLOT_TILES * P, D), F32, kind="Internal").ap() for k in range(NB)]

    with ExitStack() as ctx:
        def sb(name, shape, dt=F32):
            return ctx.enter_context(nc.sbuf_tensor(name, shape, dt))

        def sem(name):
            return ctx.enter_context(nc.semaphore(name))

        bank = [ctx.enter_context(nc.psum_tensor(f"bank{i}", [P, 512], F32)) for i in range(8)]
        def bank16(i):
            return bank[i][:, :].bitcast(F16)

        res = sb("res", [P, BATCH * TB, D])
        ident = sb("ident", [P, P])
        ident16 = sb("ident16", [P, P], F16)
        before16 = sb("before16", [P, P], F16)
        ones16 = sb("ones16", [P, P], F16)
        ones = sb("ones", [P, 1])
        iota_pos = sb("iota_pos", [P, P])
        iota_tile = sb("iota_tile", [P, SLOT_TILES])
        prio = sb("prio", [P, E])
        tok_id = sb("tok_id", [P, NT, 2])
        before_e = sb("before_e", [P, E, E])
        w1_raw = sb("w1_raw", [P, E, FF])
        w2_raw = sb("w2_raw", [P, E, CH, D])
        w1_s = sb("w1_s", [P, E, 2, FF], F16)
        w2_s = sb("w2_s", [P, E, CH, 2, D], F16)
        wr = sb("wr", [P, E])
        wqkv = sb("wqkv", [P, 3 * D])
        wout = sb("wout", [P, D])
        bias_rows = sb("bias_rows", [E * CH + 1, P])
        bias_cols = sb("bias_cols", [P, E * CH + 1])
        b_kv = sb("b_kv", [P, 2 * D])
        b_o = sb("b_o", [P, D])
        b_r = sb("b_r", [P, E])
        b_2 = sb("b_2", [P, E, D])
        stats = sb("stats", [P, NT, 6])
        mv = sb("mv", [P, NT, 2])
        rstd = sb("rstd", [P, NT])
        sq = sb("sq", [P, NT])
        root = sb("root", [P, NT])
        newt = sb("newt", [P, NT])
        xn = sb("xn", [P, NT, D])
        x_s = sb("x_s", [P, NB, NT, 2, D], F16)
        xnT = sb("xnT", [P, NT * P])
        lg = sb("lg", [P, NT, E])
        t0 = sb("t0", [P, NT, E])
        t1 = sb("t1", [P, NT, E])
        top = sb("top", [P, 2, NT])
        pr = sb("pr", [P, NT])
        oh = sb("oh", [P, 2, NT, E])
        mask16 = sb("mask16", [P, NT, E], F16)
        dlt = sb("dlt", [P, NT])
        ex = sb("ex", [P, NB, NT])
        den = sb("den", [P, NT])
        wgt = sb("wgt", [P, NB, 2, NT])
        cnt = sb("cnt", [P, E])
        cnt_i = sb("cnt_i", [P, E], I32)
        til_i = sb("til_i", [P, E], I32)
        til = sb("til", [P, E])
        t2 = sb("t2", [P, E, E])
        start = sb("start", [P, E])
        base = sb("base", [P, NT, E])
        slot = sb("slot", [P, NT, 2])
        slot_i = sb("slot_i", [P, NB, NT, 2], I32)
        sp_i = sb("sp_i", [P, 2, NT * 2], I32)
        sp_f = sb("sp_f", [P, 2, NT * 2])
        t3 = sb("t3", [P, SLOT_TILES, E])
        eid_f = sb("eid_f", [P, SLOT_TILES])
        eid = sb("eid", [P, NB, SLOT_TILES], I32)
        tile_oh = sb("tile_oh", [P, NT * 2, SLOT_TILES], F16)
        tile_id = sb("tile_id", [P, NT * 2, SLOT_TILES], F16)
        pos_oh = sb("pos_oh", [P, NT * 2, P], F16)
        ids = sb("ids", [P, NB, SLOT_TILES], I32)
        got = sb("got", [P, NG, 2 * D], F16)
        xT = sb("xT", [P, 2, 2 * D], F16)
        hid = sb("hid", [P, 2, FF])
        h_s = sb("h_s", [P, 2, 2, FF], F16)
        y_lo = sb("y_lo", [P, 2, D])
        y_sb = sb("y_sb", [P, NY, D])
        back = sb("back", [P, NT, 2, D])
        part = sb("part", [P, NT, D])
        a_xn = sb("a_xn", [P, TB, D])
        a_xT = sb("a_xT", [P, TB * P])
        q32 = sb("q32", [P, TB * P])
        q_sq = sb("q_sq", [P, TB * P])
        kv = sb("kv", [P, TB, 2 * D])
        k_sq = sb("k_sq", [P, TB, D])
        k_ss = sb("k_ss", [P, TB])
        r_k = sb("r_k", [P, TB])
        r_q = sb("r_q", [P, TB])
        kxv = sb("kxv", [P, TB, D])
        kv_sum = sb("kv_sum", [P, 1])
        wout_b = sb("wout_b", [P, D])
        res_b = sb("res_b", [P, TB, D])

        x_in = [sem(f"x_in{b}") for b in range(BATCH)]
        small_in = sem("small_in")
        bias_in = sem("bias_in")
        w1_in = [sem(f"w1_in{e}") for e in range(E)]
        w2_in = [sem(f"w2_in{e}") for e in range(E)]
        consts = sem("consts")
        w1_hi = sem("w1_hi")
        w1_lo = sem("w1_lo")
        w2_scaled = sem("w2_scaled")
        w2_hi = sem("w2_hi")
        w2_lo = sem("w2_lo")
        bias_T = sem("bias_T")
        bias_ok = sem("bias_ok")
        r_xn = sem("r_xn")
        r_hi = sem("r_hi")
        r_lo = sem("r_lo")
        r_store = [sem(f"r_store{k}") for k in range(NB)]
        r_T = sem("r_T")
        r_xT = sem("r_xT")
        r_lg = sem("r_lg")
        r_lgc = sem("r_lgc")
        r_mask = sem("r_mask")
        r_pre = sem("r_pre")
        r_pred = sem("r_pred")
        r_dlt = sem("r_dlt")
        r_ex = sem("r_ex")
        r_oh = sem("r_oh")
        r_ids = sem("r_ids")
        r_idc = sem("r_idc")
        r_eid = sem("r_eid")
        f_got = [sem(f"f_got{i}") for i in range(NG)]
        f_T = sem("f_T")
        f_xT = sem("f_xT")
        f_m1 = sem("f_m1")
        f_hid = sem("f_hid")
        f_hs = sem("f_hs")
        f_m2 = sem("f_m2")
        f_y = sem("f_y")
        f_st = [sem(f"f_st{i}") for i in range(NY)]
        c_got = [sem(f"c_got{t}") for t in range(NT)]
        c_done = sem("c_done")
        a_n = sem("a_n")
        a_T = sem("a_T")
        a_xTc = sem("a_xTc")
        a_q = sem("a_q")
        a_qe = sem("a_qe")
        a_kvm = sem("a_kvm")
        a_kv = sem("a_kv")
        a_p = sem("a_p")
        a_ss = sem("a_ss")
        a_sum = sem("a_sum")
        a_w = sem("a_w")
        a_y = sem("a_y")
        a_res = sem("a_res")
        root_of = sem("root_of")
        rooted = sem("rooted")
        chain = sem("chain")
        a_kk = sem("a_kk")
        out_st = sem("out_st")


        def stored_all(eng, n):
            done = (n + 1) * SLOT_TILES
            for i in range(NY):
                eng.wait_ge(f_st[i], 16 * ((done - i + NY - 1) // NY))

        block = ctx.enter_context(nc.Block())

        @block.sync
        def _(sp):
            for b in range(BATCH):
                sp.dma_start(res[:, b * TB:(b + 1) * TB, :], x_v[b]).then_inc(x_in[b], 16)
                if b == 0:
                    sp.dma_start(wr[:, :], w_router).then_inc(small_in, 16)
                    sp.dma_start(b_r[:, :], b_router.rearrange("(a n) -> a n", a=1).to_broadcast((P, E))).then_inc(small_in, 16)
            for e in range(E):
                sp.dma_start(w1_raw[:, e, :], w1[e]).then_inc(w1_in[e], 16)

            def store_tokens(n):
                k = n % NB
                for b in range(BB):
                    sp.wait_ge(r_lo, n * BB + b + 1)
                    sp.dma_start(tok_rows[k].rearrange("(b p j) d -> b p (j d)", b=BB, j=TB)[b],
                                 x_s[:, k, b * TB:(b + 1) * TB, :, :].rearrange("p t h d -> p (t h d)")).then_inc(r_store[k], 16)

            def store_slots(n):
                k = n % NB
                for j in range(SLOT_TILES):
                    q = n * SLOT_TILES + j
                    sp.wait_ge(f_y, q + 1)
                    sp.dma_start(slot_rows[k][j * P:(j + 1) * P, :], y_sb[:, q % NY, :]).then_inc(f_st[q % NY], 16)

            for layer in range(LAYERS):
                for k in range(NB):
                    store_tokens(layer * NB + k)
                for k in range(NB):
                    store_slots(layer * NB + k)
            for b in range(BATCH):
                sp.wait_ge(c_done, (LAYERS - 1) * BATCH + b + 1)
                sp.dma_start(out_v[b], res[:, b * TB:(b + 1) * TB, :]).then_inc(out_st, 16)
            sp.wait_ge(out_st, 16 * BATCH)

        @block.gpsimd
        def _(pool):
            g = nc.gpsimd
            g.memset(ident[:, :], 0.0).then_inc(consts, 1)
            g.memset(ones16[:, :], 1.0).then_inc(consts, 1)
            g.memset(ones[:, :], 1.0).then_inc(consts, 1)
            g.memset(t2[:, :, :], 1.0).then_inc(consts, 1)
            pool.wait_ge(consts, 4)
            g.affine_select(out=ident[:, :], in_=ident[:, :], compare_op=ALU.not_equal, fill=1.0, base=0,
                            pattern=[[-1, P]], channel_multiplier=1).then_inc(consts, 1)
            pool.wait_ge(consts, 5)
            g.tensor_copy(ident16[:, :], ident[:, :]).then_inc(consts, 1)
            g.affine_select(out=before16[:, :], in_=ones16[:, :], compare_op=ALU.is_gt, fill=0.0, base=0,
                            pattern=[[1, P]], channel_multiplier=-1).then_inc(consts, 1)
            g.affine_select(out=before_e[:, :, :], in_=t2[:, :, :], compare_op=ALU.is_gt, fill=0.0, base=0,
                            pattern=[[1, E], [-1, E]], channel_multiplier=0).then_inc(consts, 1)
            g.iota(iota_pos[:, :], [[1, P]], base=0, channel_multiplier=0,
                   allow_small_or_imprecise_dtypes=True).then_inc(consts, 1)
            g.iota(iota_tile[:, :], [[1, SLOT_TILES]], base=0, channel_multiplier=0,
                   allow_small_or_imprecise_dtypes=True).then_inc(consts, 1)
            g.iota(prio[:, :], [[-1, E]], base=E, channel_multiplier=0,
                   allow_small_or_imprecise_dtypes=True).then_inc(consts, 1)
            g.iota(tok_id[:, :, :], [[SEQ, BB], [1, TB], [0, 2]], base=0, channel_multiplier=TB,
                   allow_small_or_imprecise_dtypes=True).then_inc(consts, 1)
            for e in range(E):
                pool.wait_ge(w2_in[e], 16)
                g.tensor_scalar(w2_raw[:, e, :, :], w2_raw[:, e, :, :], W_SCALE, None, ALU.mult).then_inc(w2_scaled, 1)
            for e in range(E):
                pool.wait_ge(w2_scaled, e + 1)
                pool.wait_ge(w2_hi, e + 1)
                g.tensor_tensor(w2_s[:, e, :, 1, :], w2_raw[:, e, :, :], w2_s[:, e, :, 0, :], ALU.subtract).then_inc(w2_lo, 1)

            def dispatch(n, j):
                k, q = n % NB, n * SLOT_TILES + j
                if j == 0:
                    pool.wait_ge(r_idc, n + 1)
                    pool.wait_ge(r_store[k], 16 * BB * (n // NB + 1))
                if q >= NG:
                    pool.wait_ge(f_T, q - NG + 1)
                g.indirect_dma_start(got[:, q % NG, :], None, tok_rows[k],
                                     bass.IndirectOffsetOnAxis(ap=ids[:, k, j:j + 1], axis=0)).then_inc(f_got[q % NG], 16)

            def bring_back(n, i):
                k, t, c = n % NB, i // 2, i % 2
                if i == 0:
                    stored_all(pool, n)
                if c == 0 and n:
                    pool.wait_ge(c_done, (n - 1) * BB + t // TB + 1)
                g.indirect_dma_start(back[:, t, c, :], None, slot_rows[k],
                                     bass.IndirectOffsetOnAxis(ap=slot_i[:, k, t, c:c + 1], axis=0)).then_inc(c_got[t], 16)

            for layer in range(LAYERS):
                first, second = layer * NB, layer * NB + 1
                for j in range(SLOT_TILES):
                    dispatch(first, j)
                lead = SLOT_TILES - 2 * NT
                for j in range(SLOT_TILES):
                    dispatch(second, j)
                    if j >= lead:
                        bring_back(first, j - lead)
                for i in range(2 * NT):
                    bring_back(second, i)

        @block.scalar
        def _(act):
            s = nc.scalar
            act.dma_start(bias_rows[0:E * CH, :], b1.rearrange("e (c p) -> (e c) p", p=P)).then_inc(bias_in, 16)
            act.dma_start(bias_rows[E * CH:E * CH + 1, :], b_qkv[0:D].rearrange("(a n) -> a n", a=1)).then_inc(bias_in, 16)
            for e in range(E):
                act.dma_start(w2_raw[:, e, :, :], w2[e].rearrange("(c p) d -> p c d", p=P)).then_inc(w2_in[e], 16)
            act.dma_start(wqkv[:, :], w_qkv).then_inc(bias_in, 16)
            act.dma_start(wout[:, :], w_out).then_inc(bias_in, 16)
            act.dma_start(b_kv[:, :], b_qkv[D:3 * D].rearrange("(a n) -> a n", a=1).to_broadcast((P, 2 * D))).then_inc(bias_in, 16)
            act.dma_start(b_o[:, :], b_out.rearrange("(a n) -> a n", a=1).to_broadcast((P, D))).then_inc(bias_in, 16)
            act.dma_start(b_2[:, :, :].rearrange("p e d -> p (e d)"),
                          b2.rearrange("(a e) d -> a (e d)", a=1).to_broadcast((P, E * D))).then_inc(bias_in, 16)

            def split_weights(e):
                act.wait_ge(w1_in[e], 16)
                s.activation(w1_s[:, e, 0, :], w1_raw[:, e, :], ACT.Copy, scale=W_SCALE).then_inc(w1_hi, 1)
                act.wait_ge(w2_scaled, e + 1)
                s.activation(w2_s[:, e, :, 0, :], w2_raw[:, e, :, :], ACT.Copy).then_inc(w2_hi, 1)

            roots = [0]

            def root_act(cols):
                roots[0] += 1
                act.wait_ge(root_of, roots[0])
                s.activation(root[:, cols], sq[:, cols], ACT.Sqrt).then_inc(rooted, 1)

            def route_front(n):
                k = n % NB
                for b in range(BB):
                    root_act(slice(b * TB, (b + 1) * TB))
                for b in range(BB):
                    g0 = n * BB + b
                    tt = slice(b * TB, (b + 1) * TB)
                    act.wait_ge(r_xn, g0 + 1)
                    if n >= NB:
                        act.wait_ge(r_store[k], 16 * BB * (n // NB))
                    s.activation(x_s[:, k, tt, 0, :], xn[:, tt, :], ACT.Copy).then_inc(r_hi, 1)
                    act.wait_ge(r_T, g0 + 1)
                    if n:
                        act.wait_ge(r_lg, (n - 1) * BB + b + 1)
                    s.activation(xnT[:, b * GROUP:(b + 1) * GROUP], bank[6 + b % 2][:, :], ACT.Copy).then_inc(r_xT, 1)

            def route_exp(n):
                act.wait_ge(r_dlt, n + 1)
                s.activation(ex[:, n % NB, :], dlt[:, :], ACT.Exp).then_inc(r_ex, 1)

            def tokens_T(q):
                act.wait_ge(f_T, q + 1)
                if q >= 2:
                    act.wait_ge(f_m1, q - 1)
                s.activation(xT[:, q % 2, :], bank16(4 + q % 2)[:, 0:2 * D], ACT.Copy).then_inc(f_xT, 1)

            def hidden(q, e):
                act.wait_ge(f_m1, q + 1)
                if q >= 2:
                    act.wait_ge(f_hs, q - 1)
                for c in range(CH):
                    r = s.activation(hid[:, q % 2, c * P:(c + 1) * P], bank[q % 2][:, c * P:(c + 1) * P], ACT.Relu,
                                     bias=bias_cols[:, bass.ds(e * CH + c, 1)], scale=1.0 / W_SCALE)
                r.then_inc(f_hid, 1)

            def experts(n):
                act.wait_ge(r_eid, n + 1)
                tokens_T(n * SLOT_TILES)
                for j in range(SLOT_TILES):
                    q = n * SLOT_TILES + j
                    if j + 1 < SLOT_TILES:
                        tokens_T(q + 1)
                    e = act.value_load(eid[0:1, n % NB, j:j + 1], min_val=0, max_val=E - 1)
                    hidden(q, e)

            def attention(b):
                root_act(slice(0, TB))
                act.wait_ge(a_T, b + 1)
                if b:
                    act.wait_ge(a_kvm, b)
                s.activation(a_xT[:, :], bank[6 + b % 2][:, :], ACT.Copy).then_inc(a_xTc, 1)
                act.wait_ge(a_q, b + 1)
                if b:
                    act.wait_ge(a_y, b)
                bq = bias_cols[:, E * CH:E * CH + 1]
                s.activation(q32[:, :], bank[0][:, :], ACT.Identity, bias=bq).then_inc(a_qe, 1)
                s.activation(q_sq[:, :], bank[0][:, :], ACT.Square, bias=bq).then_inc(a_qe, 1)
                act.wait_ge(a_kv, 2 * b + 2)
                if b:
                    act.wait_ge(a_kk, TB * b)
                for t in range(TB):
                    s.activation(k_sq[:, t, :], kv[:, t, 0:D], ACT.Square, accum_out=k_ss[:, t:t + 1]).then_inc(a_kk, 1)
                root_act(slice(0, TB))
                root_act(slice(0, TB))

            act.wait_ge(bias_T, 1)
            s.activation(bias_cols[:, :], bank[5][:, 0:E * CH + 1], ACT.Copy).then_inc(bias_ok, 1)
            act.wait_ge(bias_ok, 1)
            route_front(0)
            for e in range(E // 2):
                split_weights(e)
            route_exp(0)
            route_front(1)
            for e in range(E // 2, E):
                split_weights(e)
            route_exp(1)
            experts(0)
            experts(1)
            for k in range(NB):
                for b in range(BB):
                    attention(k * BB + b)
                route_front(NB + k)
                route_exp(NB + k)
            experts(NB)
            experts(NB + 1)

        @block.vector
        def _(dve):
            v = nc.vector
            count = [0]

            def link(ins):
                count[0] += 1
                ins.then_inc(chain, 1)
                dve.wait_ge(chain, count[0])

            roots = [0]

            def inverse_root(dst, cols):
                roots[0] += 1
                dve.wait_ge(rooted, roots[0])
                link(v.reciprocal(dst, root[:, cols]))
                link(v.tensor_tensor(newt[:, cols], dst, dst, ALU.mult))
                link(v.scalar_tensor_tensor(out=newt[:, cols], in0=newt[:, cols], scalar=-0.5, in1=sq[:, cols],
                                            op0=ALU.mult, op1=ALU.mult))
                return v.scalar_tensor_tensor(out=dst, in0=newt[:, cols], scalar=1.5, in1=dst, op0=ALU.add, op1=ALU.mult)

            def moments(src, tiles):
                cols = slice(tiles[0], tiles[-1] + 1)
                for t in tiles:
                    r = v.bn_stats(stats[:, t, :], src(t))
                link(r)
                for t in tiles:
                    r = v.bn_aggr(mv[:, t, :], stats[:, t, :])
                link(r)
                v.tensor_scalar(sq[:, cols], mv[:, cols, 1], EPS, None, ALU.add).then_inc(root_of, 1)

            def normalise(src, tiles, dst, done):
                cols = slice(tiles[0], tiles[-1] + 1)
                link(inverse_root(rstd[:, cols], cols))
                for t in tiles:
                    r = v.tensor_scalar(dst(t), src(t), mv[:, t, 0:1], rstd[:, t:t + 1], ALU.subtract, ALU.mult)
                r.then_inc(done, 1)

            def route_front(n):
                k, layer = n % NB, n // NB
                for b in range(BB):
                    if layer == 0:
                        dve.wait_ge(x_in[k * BB + b], 16)
                    moments(lambda t: res[:, k * NT + t, :], range(b * TB, (b + 1) * TB))
                for b in range(BB):
                    if n:
                        dve.wait_ge(r_T, (n - 1) * BB + b + 1)
                        dve.wait_ge(r_hi, (n - 1) * BB + b + 1)
                        dve.wait_ge(r_lo, (n - 1) * BB + b + 1)
                    normalise(lambda t: res[:, k * NT + t, :], range(b * TB, (b + 1) * TB), lambda t: xn[:, t, :], r_xn)
                for b in range(BB):
                    g0 = n * BB + b
                    tt = slice(b * TB, (b + 1) * TB)
                    dve.wait_ge(r_hi, g0 + 1)
                    dve.wait_ge(r_xn, g0 + 1)
                    v.tensor_tensor(x_s[:, k, tt, 1, :], xn[:, tt, :], x_s[:, k, tt, 0, :], ALU.subtract).then_inc(r_lo, 1)

            def choose(n):
                k = n % NB
                pri = prio[:, :].unsqueeze(1).to_broadcast((P, NT, E))
                dve.wait_ge(r_lg, (n + 1) * BB)
                link(v.tensor_tensor(lg[:, :, :], bank[4][:, 0:NT * E].rearrange("p (t e) -> p t e", e=E),
                                     b_r[:, :].unsqueeze(1).to_broadcast((P, NT, E)), ALU.add))
                for c in range(2):
                    link(v.tensor_reduce(top[:, c, :], lg[:, :, :], AX_X, ALU.max))
                    link(v.tensor_tensor(t0[:, :, :], lg[:, :, :], top[:, c, :].unsqueeze(2).to_broadcast((P, NT, E)), ALU.is_equal))
                    link(v.tensor_tensor(t1[:, :, :], t0[:, :, :], pri, ALU.mult))
                    link(v.tensor_reduce(pr[:, :], t1[:, :, :], AX_X, ALU.max))
                    link(v.tensor_tensor(oh[:, c, :, :], pri, pr[:, :].unsqueeze(2).to_broadcast((P, NT, E)), ALU.is_equal))
                    if c == 0:
                        link(v.scalar_tensor_tensor(out=lg[:, :, :], in0=oh[:, 0, :, :], scalar=FAR, in1=lg[:, :, :],
                                                    op0=ALU.mult, op1=ALU.add))
                v.tensor_tensor(mask16[:, :, :], oh[:, 0, :, :], oh[:, 1, :, :], ALU.add).then_inc(r_mask, 1)
                v.tensor_tensor(dlt[:, :], top[:, 1, :], top[:, 0, :], ALU.subtract).then_inc(r_dlt, 1)

            def weights(n):
                k = n % NB
                dve.wait_ge(r_ex, n + 1)
                link(v.tensor_scalar(den[:, :], ex[:, k, :], 1.0, None, ALU.add))
                link(v.reciprocal(den[:, :], den[:, :]))
                v.tensor_scalar(wgt[:, k, 0, :], den[:, :], 0.5, None, ALU.mult)
                link(v.scalar_tensor_tensor(out=wgt[:, k, 1, :], in0=den[:, :], scalar=0.5, in1=ex[:, k, :],
                                            op0=ALU.mult, op1=ALU.mult))

            def place(n):
                k = n % NB
                dve.wait_ge(r_pre, n + 1)
                link(v.tensor_scalar(cnt_i[:, :], bank[4][:, 256:256 + E], float(P - 1), None, ALU.add))
                link(v.tensor_scalar(til_i[:, :], cnt_i[:, :], 7, None, ALU.arith_shift_right))
                link(v.tensor_copy(til[:, :], til_i[:, :]))
                link(v.tensor_tensor(t2[:, :, :], before_e[:, :, :], til[:, :].unsqueeze(1).to_broadcast((P, E, E)), ALU.mult))
                link(v.tensor_reduce(start[:, :], t2[:, :, :], AX_X, ALU.add))
                link(v.scalar_tensor_tensor(out=base[:, :, :], in0=start[:, :].unsqueeze(1).to_broadcast((P, NT, E)), scalar=float(P),
                                            in1=bank[5][:, 0:NT * E].rearrange("p (t e) -> p t e", e=E),
                                            op0=ALU.mult, op1=ALU.add))
                for c, t in ((0, t0), (1, t1)):
                    link(v.tensor_tensor(t[:, :, :], oh[:, c, :, :], base[:, :, :], ALU.mult))
                    link(v.tensor_reduce(slot[:, :, c], t[:, :, :], AX_X, ALU.add))
                link(v.tensor_copy(slot_i[:, k, :, :], slot[:, :, :]))
                flat = slot_i[:, k, :, :].rearrange("p t c -> p (t c)")
                v.tensor_scalar(sp_i[:, 0, :], flat, 7, None, ALU.arith_shift_right)
                link(v.tensor_scalar(sp_i[:, 1, :], flat, P - 1, None, ALU.bitwise_and))
                link(v.tensor_copy(sp_f[:, :, :], sp_i[:, :, :]))
                I = 2 * NT
                if n:
                    dve.wait_ge(r_ids, n)
                v.tensor_tensor(pos_oh[:, :, :], iota_pos[:, :].unsqueeze(1).to_broadcast((P, I, P)),
                                sp_f[:, 1, :].unsqueeze(2).to_broadcast((P, I, P)), ALU.is_equal).then_inc(r_oh, 1)
                link(v.tensor_tensor(tile_oh[:, :, :], iota_tile[:, :].unsqueeze(1).to_broadcast((P, I, SLOT_TILES)),
                                     sp_f[:, 0, :].unsqueeze(2).to_broadcast((P, I, SLOT_TILES)), ALU.is_equal))
                v.tensor_tensor(tile_id[:, :, :], tile_oh[:, :, :],
                                tok_id[:, :, :].rearrange("p t c -> p (t c)").unsqueeze(2).to_broadcast((P, I, SLOT_TILES)),
                                ALU.mult).then_inc(r_oh, 1)
                link(v.tensor_tensor(t3[:, :, :], iota_tile[:, :].unsqueeze(2).to_broadcast((P, SLOT_TILES, E)),
                                     start[:, :].unsqueeze(1).to_broadcast((P, SLOT_TILES, E)), ALU.is_ge))
                link(v.tensor_reduce(eid_f[:, :], t3[:, :, :], AX_X, ALU.add))
                v.tensor_scalar(eid[:, k, :], eid_f[:, :], -1.0, None, ALU.add).then_inc(r_eid, 1)
                dve.wait_ge(r_ids, n + 1)
                v.tensor_copy(ids[:, k, :], bank[5][:, 256:256 + SLOT_TILES]).then_inc(r_idc, 1)

            def split_hidden(q):
                dve.wait_ge(f_hid, q + 1)
                if q >= 2:
                    dve.wait_ge(f_m2, q - 1)
                link(v.tensor_copy(h_s[:, q % 2, 0, :], hid[:, q % 2, :]))
                v.tensor_tensor(h_s[:, q % 2, 1, :], hid[:, q % 2, :], h_s[:, q % 2, 0, :], ALU.subtract).then_inc(f_hs, 1)

            def expert_out(q, e):
                dve.wait_ge(f_m2, q + 1)
                if q >= 2:
                    dve.wait_ge(f_y, q - 1)
                ps = bank[2 + q % 2]
                link(v.scalar_tensor_tensor(out=y_lo[:, q % 2, :], in0=ps[:, D:2 * D], scalar=1.0 / W_SCALE,
                                            in1=b_2[:, bass.ds(e, 1), :].rearrange("p a d -> p (a d)"),
                                            op0=ALU.mult, op1=ALU.add))
                if q >= NY:
                    dve.wait_ge(f_st[q % NY], 16 * (q // NY))
                v.scalar_tensor_tensor(out=y_sb[:, q % NY, :], in0=ps[:, 0:D], scalar=1.0 / W_SCALE, in1=y_lo[:, q % 2, :],
                                       op0=ALU.mult, op1=ALU.add).then_inc(f_y, 1)

            def experts(n):
                split_hidden(n * SLOT_TILES)
                for j in range(SLOT_TILES):
                    q = n * SLOT_TILES + j
                    if j + 1 < SLOT_TILES:
                        split_hidden(q + 1)
                    e = dve.value_load(eid[0:1, n % NB, j:j + 1], min_val=0, max_val=E - 1)
                    expert_out(q, e)

            def combine(n, b):
                k = n % NB
                for t in range(b * TB, (b + 1) * TB):
                    dve.wait_ge(c_got[t], 32 * (n + 1))
                    v.scalar_tensor_tensor(out=part[:, t, :], in0=back[:, t, 0, :], scalar=wgt[:, k, 0, t:t + 1],
                                           in1=res[:, k * NT + t, :], op0=ALU.mult, op1=ALU.add).then_inc(chain, 1)
                    count[0] += 1
                dve.wait_ge(chain, count[0])
                for t in range(b * TB, (b + 1) * TB):
                    r = v.scalar_tensor_tensor(out=res[:, k * NT + t, :], in0=back[:, t, 1, :], scalar=wgt[:, k, 1, t:t + 1],
                                               in1=part[:, t, :], op0=ALU.mult, op1=ALU.add)
                r.then_inc(c_done, 1)

            def attention(b):
                rt = slice(b * TB, (b + 1) * TB)
                cols = slice(0, TB)
                moments(lambda t: res[:, b * TB + t, :], range(TB))
                if b:
                    dve.wait_ge(a_T, b)
                normalise(lambda t: res[:, b * TB + t, :], range(TB), lambda t: a_xn[:, t, :], a_n)
                v.tensor_tensor(res_b[:, :, :], res[:, rt, :], b_o[:, :].unsqueeze(1).to_broadcast((P, TB, D)), ALU.add)
                for h in range(2):
                    dve.wait_ge(a_kvm, b + 1)
                    v.tensor_tensor(kv[:, 2 * h:2 * h + 2, :], bank[1 + h][:, :].rearrange("p (t n) -> p t n", t=2),
                                    b_kv[:, :].unsqueeze(1).to_broadcast((P, 2, 2 * D)), ALU.add).then_inc(a_kv, 1)
                dve.wait_ge(a_kv, 2 * b + 2)
                if b:
                    dve.wait_ge(a_sum, b)
                link(v.tensor_tensor(kxv[:, :, :], kv[:, :, 0:D], kv[:, :, D:2 * D], ALU.mult))
                dve.wait_ge(a_kk, TB * (b + 1))
                v.tensor_copy(sq[:, cols], k_ss[:, :]).then_inc(root_of, 1)
                inverse_root(r_k[:, :], cols).then_inc(a_p, 1)
                dve.wait_ge(a_p, b + 1)
                dve.wait_ge(a_ss, b + 1)
                v.tensor_copy(sq[:, cols], bank[3][:, 0:TB]).then_inc(root_of, 1)
                link(inverse_root(r_q[:, :], cols))
                dve.wait_ge(a_sum, b + 1)
                link(v.tensor_copy(kv_sum[:, :], bank[4][:, 0:1]))
                if b:
                    dve.wait_ge(a_y, b)
                v.tensor_scalar(wout_b[:, :], wout[:, :], kv_sum[:, 0:1], None, ALU.mult).then_inc(a_w, 1)
                dve.wait_ge(a_y, b + 1)
                for t in range(TB):
                    r = v.scalar_tensor_tensor(out=res[:, b * TB + t, :], in0=bank[5][:, t * D:(t + 1) * D],
                                               scalar=r_q[:, t:t + 1], in1=res_b[:, t, :], op0=ALU.mult, op1=ALU.add)
                r.then_inc(a_res, 1)
                dve.wait_ge(a_res, b + 1)

            def split_w1(e):
                dve.wait_ge(w1_hi, e + 1)
                v.scalar_tensor_tensor(out=w1_s[:, e, 1, :], in0=w1_raw[:, e, :], scalar=W_SCALE,
                                       in1=w1_s[:, e, 0, :], op0=ALU.mult, op1=ALU.subtract).then_inc(w1_lo, 1)

            dve.wait_ge(consts, 12)
            dve.wait_ge(small_in, 32)
            for n in range(NB):
                route_front(n)
                choose(n)
                place(n)
                weights(n)
                for e in range(n * E // NB, (n + 1) * E // NB):
                    split_w1(e)
            experts(0)
            dve.wait_ge(bias_in, 16 * 7)
            experts(1)
            for k in range(NB):
                for b in range(BB):
                    combine(k, b)
                    dve.wait_ge(c_done, k * BB + b + 1)
                    attention(k * BB + b)
                route_front(NB + k)
                choose(NB + k)
                place(NB + k)
                weights(NB + k)
            for k in range(NB):
                experts(NB + k)
            for k in range(NB):
                for b in range(BB):
                    combine(NB + k, b)

        @block.tensor
        def _(pe):
            mm = nc.tensor.matmul

            def route_logits(n):
                for b in range(BB):
                    g0 = n * BB + b
                    pe.wait_ge(r_xn, g0 + 1)
                    if n:
                        pe.wait_ge(r_xT, (n - 1) * BB + b + 1)
                    for t in range(TB):
                        r = nc.tensor.transpose(bank[6 + b % 2][:, t * P:(t + 1) * P], xn[:, b * TB + t, :], ident[:, :])
                    r.then_inc(r_T, 1)
                for b in range(BB):
                    g0 = n * BB + b
                    pe.wait_ge(r_xT, g0 + 1)
                    for t in range(b * TB, (b + 1) * TB):
                        r = mm(bank[4][:, t * E:(t + 1) * E], xnT[:, t * P:(t + 1) * P], wr[:, :], start=True, stop=True)
                    r.then_inc(r_lg, 1)

            def route_place(n):
                pe.wait_ge(r_mask, n + 1)
                m = mask16[:, :, :].rearrange("p t e -> p (t e)")
                mm(bank[5][:, 0:NT * E], before16[:, :], m, start=True, stop=False, skip_group_check=True)
                for s in range(1, NT):
                    mm(bank[5][:, s * E:NT * E], ones16[:, :], m[:, 0:(NT - s) * E], start=False, stop=(s == NT - 1), skip_group_check=True)
                for t in range(NT):
                    r = mm(bank[4][:, 256:256 + E], ones16[:, :], m[:, t * E:(t + 1) * E], start=(t == 0), stop=(t == NT - 1))
                r.then_inc(r_pre, 1)
                pe.wait_ge(r_oh, 2 * (n + 1))
                for i in range(2 * NT):
                    r = mm(bank[5][:, 256:256 + SLOT_TILES], pos_oh[:, i, :], tile_id[:, i, :], start=(i == 0), stop=(i == 2 * NT - 1))
                r.then_inc(r_ids, 1)

            def tokens_T(q):
                pe.wait_ge(f_got[q % NG], 16 * (q // NG + 1))
                if q >= 2:
                    pe.wait_ge(f_xT, q - 1)
                for h in range(2):
                    r = nc.tensor.transpose(bank16(4 + q % 2)[:, h * D:(h + 1) * D], got[:, q % NG, h * D:(h + 1) * D], ident16[:, :])
                r.then_inc(f_T, 1)

            def product1(q, e):
                pe.wait_ge(f_xT, q + 1)
                if q >= 2:
                    pe.wait_ge(f_hid, q - 1)
                x_hi, x_lo = xT[:, q % 2, 0:D], xT[:, q % 2, D:2 * D]
                for c in range(CH):
                    o = bank[q % 2][:, c * P:(c + 1) * P]
                    w = [w1_s[:, bass.ds(e, 1), h, c * P:(c + 1) * P].rearrange("p a f -> p (a f)") for h in range(2)]
                    mm(o, w[0], x_hi, start=True, stop=False)
                    mm(o, w[0], x_lo, start=False, stop=False)
                    r = mm(o, w[1], x_hi, start=False, stop=True)
                r.then_inc(f_m1, 1)

            def product2(q, e):
                pe.wait_ge(f_hs, q + 1)
                if q >= 2:
                    pe.wait_ge(f_y, q - 1)
                o = bank[2 + q % 2]
                for c in range(CH):
                    w = w2_s[:, bass.ds(e, 1), c, :, :].rearrange("p a h d -> p (a h d)")
                    mm(o[:, 0:2 * D], h_s[:, q % 2, 0, c * P:(c + 1) * P], w, start=(c == 0), stop=False, skip_group_check=True)
                    r = mm(o[:, 0:D], h_s[:, q % 2, 1, c * P:(c + 1) * P], w[:, 0:D], start=False, stop=(c == CH - 1), skip_group_check=True)
                r.then_inc(f_m2, 1)

            def experts(n):
                q0, k = n * SLOT_TILES, n % NB
                pe.wait_ge(r_eid, n + 1)
                pe.wait_ge(r_idc, (n // NB + 1) * NB)
                tokens_T(q0)
                e_next = pe.value_load(eid[0:1, k, 0:1], min_val=0, max_val=E - 1)
                tokens_T(q0 + 1)
                product1(q0, e_next)
                for j in range(SLOT_TILES):
                    e = e_next
                    if j + 2 < SLOT_TILES:
                        tokens_T(q0 + j + 2)
                    if j + 1 < SLOT_TILES:
                        e_next = pe.value_load(eid[0:1, k, j + 1:j + 2], min_val=0, max_val=E - 1)
                        product1(q0 + j + 1, e_next)
                    product2(q0 + j, e)

            def attention(b):
                pe.wait_ge(a_n, b + 1)
                if b >= 2:
                    pe.wait_ge(a_xTc, b - 1)
                for t in range(TB):
                    r = nc.tensor.transpose(bank[6 + b % 2][:, t * P:(t + 1) * P], a_xn[:, t, :], ident[:, :])
                r.then_inc(a_T, 1)
                pe.wait_ge(a_xTc, b + 1)
                if b:
                    pe.wait_ge(a_qe, 2 * b)
                    pe.wait_ge(a_kv, 2 * b)
                mm(bank[0][:, :], wqkv[:, 0:D], a_xT[:, :], start=True, stop=True).then_inc(a_q, 1)
                for t in range(TB):
                    r = mm(bank[1 + t // 2][:, (t % 2) * 2 * D:(t % 2 + 1) * 2 * D], a_xT[:, t * P:(t + 1) * P], wqkv[:, D:3 * D],
                           start=True, stop=True)
                r.then_inc(a_kvm, 1)
                pe.wait_ge(a_qe, 2 * b + 2)
                if b:
                    pe.wait_ge(a_res, b)
                for t in range(TB):
                    r = mm(bank[3][:, t:t + 1], q_sq[:, t * P:(t + 1) * P], ones[:, :], start=True, stop=True)
                r.then_inc(a_ss, 1)
                pe.wait_ge(a_p, b + 1)
                for t in range(TB):
                    r = mm(bank[4][:, 0:1], kxv[:, t, :], r_k[:, t:t + 1], start=(t == 0), stop=(t == TB - 1))
                r.then_inc(a_sum, 1)
                pe.wait_ge(a_w, b + 1)
                for t in range(TB):
                    r = mm(bank[5][:, t * D:(t + 1) * D], q32[:, t * P:(t + 1) * P], wout_b[:, :], start=True, stop=True)
                r.then_inc(a_y, 1)

            pe.wait_ge(consts, 12)
            pe.wait_ge(bias_in, 16 * 7)
            R = E * CH + 1
            nc.tensor.transpose(bank[5][:, 0:R], bias_rows[:, :], ident[0:R, 0:R]).then_inc(bias_T, 1)
            pe.wait_ge(small_in, 32)
            pe.wait_ge(bias_ok, 1)
            for n in range(NB):
                if n:
                    pe.wait_ge(r_idc, n)
                route_logits(n)
                route_place(n)
            pe.wait_ge(w1_lo, E)
            pe.wait_ge(w2_lo, E)
            experts(0)
            experts(1)
            for k in range(NB):
                for b in range(BB):
                    n = k * BB + b
                    if n == 0:
                        pe.wait_ge(f_y, NB * SLOT_TILES)
                    elif b == 0:
                        pe.wait_ge(r_idc, NB + k)
                    attention(n)
                pe.wait_ge(a_res, (k + 1) * BB)
                route_logits(NB + k)
                route_place(NB + k)
            for k in range(NB):
                experts(NB + k)


_INS = ['L0_attn_x', 'L0_attn_Wqkv', 'L0_attn_bqkv', 'L0_attn_Wout', 'L0_attn_bout', 'L0_ffn_W_router',
        'L0_ffn_b_router', 'L0_ffn_W1', 'L0_ffn_b1', 'L0_ffn_W2', 'L0_ffn_b2']


def kernel(**inputs):
    import numpy as _np
    import concourse.bacc as _bacc
    from concourse import mybir as _mybir
    from concourse.bass_utils import run_bass_kernel_spmd as _run

    nc = _bacc.Bacc("TRN2", target_bir_lowering=False, num_devices=1)
    arrays, args = {}, []
    for name in _INS:
        a = _np.ascontiguousarray(inputs[name])
        arrays[f"in_{name}"] = a
        args.append(nc.dram_tensor(f"in_{name}", a.shape, _mybir.dt.from_np(a.dtype), kind="ExternalInput").ap())
    args.append(nc.dram_tensor("out_0", inputs['L0_attn_x'].shape, _mybir.dt.float32, kind="ExternalOutput").ap())
    macaron(nc, *args)
    r = _run(nc, [arrays], core_ids=[0])
    return r.results[0]["out_0"]
```

```python
from contextlib import ExitStack

import concourse.bass as bass
from concourse import mybir

P = 128
F32 = mybir.dt.float32
F16 = mybir.dt.float16
I32 = mybir.dt.int32
ALU = mybir.AluOpType
ACT = mybir.ActivationFunctionType
AX_X = mybir.AxisListType.X
EPS = 1e-5
W_SCALE = 64.0
FAR = -3.0e38


def macaron(nc, x, w_qkv, b_qkv, w_out, b_out, w_router, b_router, w1, b1, w2, b2, out):
    BATCH, SEQ, D = x.shape
    E, _, FF = w1.shape
    CH = FF // P
    TB = SEQ // P
    NB = 1
    LAYERS = 2
    BB = BATCH // NB
    NT = BB * TB
    BLOCK = NT * P
    SLOT_TILES = (2 * BLOCK + E * (P - 1)) // P
    GROUP = TB * D
    NG, NY = 8, 4
    LEAD = 5
    assert D == P and BATCH % NB == 0

    x_v = x.rearrange("b (p j) d -> b p j d", j=TB)
    out_v = out.rearrange("b (p j) d -> b p j d", j=TB)
    tok_rows = [nc.dram_tensor(f"tok_rows{k}", (BLOCK, 2 * D), F16, kind="Internal").ap() for k in range(NB)]
    pair_rows = [nc.dram_tensor(f"pair_rows{k}", (2 * BLOCK, D), F32, kind="Internal").ap() for k in range(NB)]

    with ExitStack() as ctx:
        def sb(name, shape, dt=F32):
            return ctx.enter_context(nc.sbuf_tensor(name, shape, dt))

        def sem(name):
            return ctx.enter_context(nc.semaphore(name))

        bank = [ctx.enter_context(nc.psum_tensor(f"bank{i}", [P, 512], F32)) for i in range(8)]
        def bank16(i):
            return bank[i][:, :].bitcast(F16)

        res = sb("res", [P, BATCH * TB, D])
        ident = sb("ident", [P, P])
        ident16 = sb("ident16", [P, P], F16)
        before16 = sb("before16", [P, P], F16)
        ones16 = sb("ones16", [P, P], F16)
        ones = sb("ones", [P, 1])
        iota_pos = sb("iota_pos", [P, P])
        iota_tile = sb("iota_tile", [P, SLOT_TILES])
        iota16 = sb("iota16", [P, P], F16)
        prio = sb("prio", [P, E])
        tok_id = sb("tok_id", [P, NT, 2])
        choice = sb("choice", [P, NT, 2])
        before_e = sb("before_e", [P, E, E])
        w1_raw = sb("w1_raw", [P, E, FF])
        w2_raw = sb("w2_raw", [P, E, CH, D])
        w1_s = sb("w1_s", [P, E, 2, FF], F16)
        w2_s = sb("w2_s", [P, E, CH, 2, D], F16)
        wr = sb("wr", [P, E])
        wqkv = sb("wqkv", [P, 3 * D])
        wout = sb("wout", [P, D])
        bias_rows = sb("bias_rows", [E * CH + 1, P])
        bias_cols = sb("bias_cols", [P, E * CH + 1])
        b_kv = sb("b_kv", [P, 2 * D])
        b_o = sb("b_o", [P, D])
        b_r = sb("b_r", [P, E])
        b_2 = sb("b_2", [P, E, D])
        stats = sb("stats", [P, 2 * NT, 6])
        mv = sb("mv", [P, 2 * NT, 2])
        rstd = sb("rstd", [P, 4 * NT])
        shift = sb("shift", [P, 2 * NT])
        sq = sb("sq", [P, 4 * NT])
        root = sb("root", [P, 4 * NT])
        xn = sb("xn", [P, NT, D])
        x_s = sb("x_s", [P, NB, NT, 2, D], F16)
        xnT = sb("xnT", [P, NT * P])
        lg = sb("lg", [P, NT, E])
        t0 = sb("t0", [P, NT, E])
        t1 = sb("t1", [P, NT, E])
        top = sb("top", [P, 2, NT])
        pr = sb("pr", [P, NT])
        oh = sb("oh", [P, 2, NT, E])
        mask16 = sb("mask16", [P, NT, E], F16)
        dlt = sb("dlt", [P, NT])
        ex = sb("ex", [P, NB, NT])
        den = sb("den", [P, NT])
        wgt = sb("wgt", [P, NB, 2, NT])
        cnt = sb("cnt", [P, E])
        cnt_i = sb("cnt_i", [P, E], I32)
        til_i = sb("til_i", [P, E], I32)
        til = sb("til", [P, E])
        t2 = sb("t2", [P, E, E])
        start = sb("start", [P, E])
        base = sb("base", [P, NT, E])
        slot = sb("slot", [P, NT, 2])
        slot_i = sb("slot_i", [P, NB, NT, 2], I32)
        sp_i = sb("sp_i", [P, 2, NT * 2], I32)
        sp_f = sb("sp_f", [P, 2, NT * 2])
        t3 = sb("t3", [P, SLOT_TILES, E])
        eid_f = sb("eid_f", [P, SLOT_TILES])
        eid = sb("eid", [P, NB, SLOT_TILES], I32)
        tile_oh = sb("tile_oh", [P, NT * 2, SLOT_TILES], F16)
        tile_id = sb("tile_id", [P, NT * 2, 2, SLOT_TILES], F16)
        pos_oh = sb("pos_oh", [P, NT * 2, P], F16)
        ids = sb("ids", [P, NB, SLOT_TILES], I32)
        ids_f = sb("ids_f", [P, SLOT_TILES])
        dest_f = sb("dest_f", [P, SLOT_TILES])
        dest = sb("dest", [P, NB, SLOT_TILES], I32)
        got = sb("got", [P, NG, 2 * D], F16)
        xT = sb("xT", [P, 2, 2 * D], F16)
        hid = sb("hid", [P, 2, FF])
        h_s = sb("h_s", [P, 2, 2, FF], F16)
        y_lo = sb("y_lo", [P, 2, D])
        y_sb = sb("y_sb", [P, NY, D])
        back = sb("back", [P, BB, 2, TB, D])
        part = sb("part", [P, NT, D])
        a_xn = sb("a_xn", [P, 2, TB, D])
        a_xT = sb("a_xT", [P, TB * P])
        q32 = sb("q32", [P, 2, TB * P])
        q_sq = sb("q_sq", [P, 2, TB * P])
        kv = sb("kv", [P, TB, 2 * D])
        k_sq = sb("k_sq", [P, TB, D])
        kxv = sb("kxv", [P, 2, TB, D])
        kv_sum = sb("kv_sum", [P, 1])
        wout_b = sb("wout_b", [P, D])
        res_b = sb("res_b", [P, BATCH, TB, D])

        x_in = [sem(f"x_in{b}") for b in range(BATCH)]
        small_in = sem("small_in")
        bias_in = sem("bias_in")
        w1_in = [sem(f"w1_in{e}") for e in range(E)]
        w2_in = [sem(f"w2_in{e}") for e in range(E)]
        consts = sem("consts")
        w1_hi = sem("w1_hi")
        w1_lo = sem("w1_lo")
        w2_scaled = sem("w2_scaled")
        w2_hi = sem("w2_hi")
        w2_lo = sem("w2_lo")
        bias_T = sem("bias_T")
        bias_ok = sem("bias_ok")
        r_xn = sem("r_xn")
        r_hi = sem("r_hi")
        r_lo = sem("r_lo")
        r_store = [sem(f"r_store{k}") for k in range(NB)]
        r_T = sem("r_T")
        r_xT = sem("r_xT")
        r_lg = sem("r_lg")
        r_lgc = sem("r_lgc")
        r_mask = sem("r_mask")
        r_pre = sem("r_pre")
        r_pred = sem("r_pred")
        r_toh = sem("r_toh")
        r_dlt = sem("r_dlt")
        r_ex = sem("r_ex")
        r_oh = sem("r_oh")
        r_ids = sem("r_ids")
        r_idc = sem("r_idc")
        r_eid = sem("r_eid")
        f_got = [sem(f"f_got{i}") for i in range(NG)]
        f_T = sem("f_T")
        f_xT = sem("f_xT")
        f_m1 = sem("f_m1")
        f_hid = sem("f_hid")
        f_hs = sem("f_hs")
        f_m2 = sem("f_m2")
        f_y = sem("f_y")
        f_st = [sem(f"f_st{i}") for i in range(NY)]
        c_got = [sem(f"c_got{b}") for b in range(BB)]
        c_done = sem("c_done")
        a_s = sem("a_s")
        r_s = sem("r_s")
        a_n = sem("a_n")
        a_T = sem("a_T")
        a_xTc = sem("a_xTc")
        a_q = sem("a_q")
        a_qe = sem("a_qe")
        a_kvm = sem("a_kvm")
        a_kv = sem("a_kv")
        a_p = sem("a_p")
        a_ss = sem("a_ss")
        a_sum = sem("a_sum")
        a_w = sem("a_w")
        a_y = sem("a_y")
        a_res = sem("a_res")
        a_rk = sem("a_rk")
        a_rq = sem("a_rq")
        a_rb = sem("a_rb")
        root_of = sem("root_of")
        rooted = sem("rooted")
        chain = sem("chain")
        a_kk = sem("a_kk")
        out_st = sem("out_st")


        def stored_all(eng, n):
            done = (n + 1) * SLOT_TILES
            for i in range(NY):
                eng.wait_ge(f_st[i], 16 * ((done - i + NY - 1) // NY))

        LOAD = 8

        def load_experts(engine, n, j):
            return nc.values_load_multi_w_load_instructions(
                eid[0:1, n % NB, j:min(j + LOAD, SLOT_TILES)], engines=(engine,), min_val=0, max_val=E - 1,
                skip_runtime_bounds_check_because="an expert is a count of at most E starts, less one")[1]

        block = ctx.enter_context(nc.Block())

        @block.sync
        def _(sp):
            for b in range(BATCH):
                sp.dma_start(res[:, b * TB:(b + 1) * TB, :], x_v[b]).then_inc(x_in[b], 16)
                if b == 0:
                    sp.dma_start(wr[:, :], w_router).then_inc(small_in, 16)
                    sp.dma_start(b_r[:, :], b_router.rearrange("(a n) -> a n", a=1).to_broadcast((P, E))).then_inc(small_in, 16)
            for e in range(E):
                sp.dma_start(w1_raw[:, e, :], w1[e]).then_inc(w1_in[e], 16)

            def store_tokens(n):
                k = n % NB
                for b in range(BB):
                    sp.wait_ge(r_lo, n * BB + b + 1)
                    sp.dma_start(tok_rows[k].rearrange("(b p j) d -> b p (j d)", b=BB, j=TB)[b],
                                 x_s[:, k, b * TB:(b + 1) * TB, :, :].rearrange("p t h d -> p (t h d)")).then_inc(r_store[k], 16)

            def fetch_pairs(n):
                k = n % NB
                stored_all(sp, n)
                rows = pair_rows[k].rearrange("(c b p j) d -> b p c (j d)", c=2, b=BB, j=TB)
                for b in range(BB):
                    if n >= NB:
                        sp.wait_ge(c_done, (n - NB) * BB + b + 1)
                    sp.dma_start(back[:, b, :, :, :].rearrange("p c j d -> p c (j d)"), rows[b]).then_inc(c_got[b], 16)

            for n in range(LAYERS * NB):
                store_tokens(n)
                fetch_pairs(n)
            for b in range(BATCH):
                sp.wait_ge(c_done, (LAYERS - 1) * BATCH + b + 1)
                sp.dma_start(out_v[b], res[:, b * TB:(b + 1) * TB, :]).then_inc(out_st, 16)
            sp.wait_ge(out_st, 16 * BATCH)

        @block.gpsimd
        def _(pool):
            g = nc.gpsimd
            g.memset(ident[:, :], 0.0).then_inc(consts, 1)
            g.memset(ones16[:, :], 1.0).then_inc(consts, 1)
            g.memset(ones[:, :], 1.0).then_inc(consts, 1)
            g.memset(t2[:, :, :], 1.0).then_inc(consts, 1)
            pool.wait_ge(consts, 4)
            g.affine_select(out=ident[:, :], in_=ident[:, :], compare_op=ALU.not_equal, fill=1.0, base=0,
                            pattern=[[-1, P]], channel_multiplier=1).then_inc(consts, 1)
            pool.wait_ge(consts, 5)
            g.tensor_copy(ident16[:, :], ident[:, :]).then_inc(consts, 1)
            g.affine_select(out=before16[:, :], in_=ones16[:, :], compare_op=ALU.is_gt, fill=0.0, base=0,
                            pattern=[[1, P]], channel_multiplier=-1).then_inc(consts, 1)
            g.affine_select(out=before_e[:, :, :], in_=t2[:, :, :], compare_op=ALU.is_gt, fill=0.0, base=0,
                            pattern=[[1, E], [-1, E]], channel_multiplier=0).then_inc(consts, 1)
            g.iota(iota_pos[:, :], [[1, P]], base=0, channel_multiplier=0,
                   allow_small_or_imprecise_dtypes=True).then_inc(consts, 1)
            g.iota(iota_tile[:, :], [[1, SLOT_TILES]], base=0, channel_multiplier=0,
                   allow_small_or_imprecise_dtypes=True).then_inc(consts, 1)
            g.iota(prio[:, :], [[-1, E]], base=E, channel_multiplier=0,
                   allow_small_or_imprecise_dtypes=True).then_inc(consts, 1)
            g.iota(tok_id[:, :, :], [[SEQ, BB], [1, TB], [0, 2]], base=0, channel_multiplier=TB,
                   allow_small_or_imprecise_dtypes=True).then_inc(consts, 1)
            g.iota(choice[:, :, :], [[0, NT], [1, 2]], base=-2, channel_multiplier=0,
                   allow_small_or_imprecise_dtypes=True).then_inc(consts, 1)
            pool.wait_ge(consts, 13)
            g.tensor_copy(iota16[:, :], iota_pos[:, :]).then_inc(consts, 1)
            for e in range(E):
                pool.wait_ge(w2_in[e], 16)
                g.tensor_scalar(w2_raw[:, e, :, :], w2_raw[:, e, :, :], W_SCALE, None, ALU.mult).then_inc(w2_scaled, 1)
            for e in range(E):
                pool.wait_ge(w2_scaled, e + 1)
                pool.wait_ge(w2_hi, e + 1)
                g.tensor_tensor(w2_s[:, e, :, 1, :], w2_raw[:, e, :, :], w2_s[:, e, :, 0, :], ALU.subtract).then_inc(w2_lo, 1)

            def dispatch(n, j):
                k, q = n % NB, n * SLOT_TILES + j
                if j == 0:
                    pool.wait_ge(r_idc, n + 1)
                    pool.wait_ge(r_store[k], 16 * BB * (n // NB + 1))
                if q >= NG:
                    pool.wait_ge(f_T, q - NG + 1)
                g.indirect_dma_start(got[:, q % NG, :], None, tok_rows[k],
                                     bass.IndirectOffsetOnAxis(ap=ids[:, k, j:j + 1], axis=0)).then_inc(f_got[q % NG], 16)

            def give_back(n, j):
                k, q = n % NB, n * SLOT_TILES + j
                pool.wait_ge(f_y, q + 1)
                g.indirect_dma_start(pair_rows[k], bass.IndirectOffsetOnAxis(ap=dest[:, k, j:j + 1], axis=0), y_sb[:, q % NY, :],
                                     None, bounds_check=2 * BLOCK - 1, oob_is_err=False).then_inc(f_st[q % NY], 16)

            for n in range(LAYERS * NB):
                pool.wait_ge(r_toh, n + 1)
                g.tensor_tensor(tile_id[:, :, 1, :], tile_oh[:, :, :],
                                choice[:, :, :].rearrange("p t c -> p (t c)").unsqueeze(2).to_broadcast((P, 2 * NT, SLOT_TILES)),
                                ALU.mult).then_inc(r_oh, 1)
                for j in range(SLOT_TILES + LEAD):
                    if j < SLOT_TILES:
                        dispatch(n, j)
                    if j >= LEAD:
                        give_back(n, j - LEAD)

        @block.scalar
        def _(act):
            s = nc.scalar
            act.dma_start(bias_rows[0:E * CH, :], b1.rearrange("e (c p) -> (e c) p", p=P)).then_inc(bias_in, 16)
            act.dma_start(bias_rows[E * CH:E * CH + 1, :], b_qkv[0:D].rearrange("(a n) -> a n", a=1)).then_inc(bias_in, 16)
            act.dma_start(wqkv[:, :], w_qkv).then_inc(bias_in, 16)
            act.dma_start(wout[:, :], w_out).then_inc(bias_in, 16)
            act.dma_start(b_kv[:, :], b_qkv[D:3 * D].rearrange("(a n) -> a n", a=1).to_broadcast((P, 2 * D))).then_inc(bias_in, 16)
            act.dma_start(b_o[:, :], b_out.rearrange("(a n) -> a n", a=1).to_broadcast((P, D))).then_inc(bias_in, 16)
            act.dma_start(b_2[:, :, :].rearrange("p e d -> p (e d)"),
                          b2.rearrange("(a e) d -> a (e d)", a=1).to_broadcast((P, E * D))).then_inc(bias_in, 16)
            for e in range(E):
                act.dma_start(w2_raw[:, e, :, :], w2[e].rearrange("(c p) d -> p c d", p=P)).then_inc(w2_in[e], 16)

            def split_weights(e):
                act.wait_ge(w1_in[e], 16)
                s.activation(w1_s[:, e, 0, :], w1_raw[:, e, :], ACT.Copy, scale=W_SCALE).then_inc(w1_hi, 1)
                act.wait_ge(w2_scaled, e + 1)
                s.activation(w2_s[:, e, :, 0, :], w2_raw[:, e, :, :], ACT.Copy).then_inc(w2_hi, 1)

            roots = [0]

            def root_act(cols):
                roots[0] += 1
                act.wait_ge(root_of, roots[0])
                s.activation(root[:, cols], sq[:, cols], ACT.Sqrt).then_inc(rooted, 1)

            def normalise(src, dst, col, ready, waited, done):
                act.wait_ge(ready, waited)
                for t in range(TB):
                    r = s.activation(dst(t), src(t), ACT.Identity, scale=rstd[:, col + t:col + t + 1], bias=shift[:, col + t:col + t + 1])
                r.then_inc(done, 1)

            def route_root(b):
                root_act(slice(b * TB, (b + 1) * TB))

            def route_front(n, b):
                k, g0 = n % NB, n * BB + b
                tt = slice(b * TB, (b + 1) * TB)
                if n:
                    act.wait_ge(r_T, (n - 1) * BB + b + 1)
                    act.wait_ge(r_lo, (n - 1) * BB + b + 1)
                normalise(lambda t: res[:, b * TB + t, :], lambda t: xn[:, b * TB + t, :], b * TB, r_s, g0 + 1, r_xn)
                act.wait_ge(r_xn, g0 + 1)
                if n >= NB:
                    act.wait_ge(r_store[k], 16 * BB * (n // NB))
                s.activation(x_s[:, k, tt, 0, :], xn[:, tt, :], ACT.Copy).then_inc(r_hi, 1)
                act.wait_ge(r_T, g0 + 1)
                if n:
                    act.wait_ge(r_lg, (n - 1) * BB + b + 1)
                s.activation(xnT[:, b * GROUP:(b + 1) * GROUP], bank[6 + b % 2][:, :], ACT.Copy).then_inc(r_xT, 1)

            def route_exp(n):
                act.wait_ge(r_dlt, n + 1)
                s.activation(ex[:, n % NB, :], dlt[:, :], ACT.Exp).then_inc(r_ex, 1)

            def tokens_T(q):
                act.wait_ge(f_T, q + 1)
                if q >= 2:
                    act.wait_ge(f_m1, q - 1)
                s.activation(xT[:, q % 2, :], bank16(4 + q % 2)[:, 0:2 * D], ACT.Copy).then_inc(f_xT, 1)

            def hidden(q, e):
                act.wait_ge(f_m1, q + 1)
                if q >= 2:
                    act.wait_ge(f_hs, q - 1)
                for c in range(CH):
                    r = s.activation(hid[:, q % 2, c * P:(c + 1) * P], bank[q % 2][:, c * P:(c + 1) * P], ACT.Relu,
                                     bias=bias_cols[:, bass.ds(e * CH + c, 1)], scale=1.0 / W_SCALE)
                r.then_inc(f_hid, 1)

            def experts(n):
                act.wait_ge(r_eid, n + 1)
                tokens_T(n * SLOT_TILES)
                for j in range(SLOT_TILES):
                    q = n * SLOT_TILES + j
                    if j + 1 < SLOT_TILES:
                        tokens_T(q + 1)
                    if j % LOAD == 0:
                        e_of = load_experts(mybir.EngineType.Activation, n, j)
                    hidden(q, e_of[j % LOAD])

            def attend_a(b):
                root_act(slice(NT + b * TB, NT + (b + 1) * TB))
                if b >= 2:
                    act.wait_ge(a_T, b - 1)
                normalise(lambda t: res[:, b * TB + t, :], lambda t: a_xn[:, b % 2, t, :], NT + b * TB, a_s, b + 1, a_n)
                act.wait_ge(a_T, b + 1)
                if b:
                    act.wait_ge(a_q, b)
                s.activation(a_xT[:, :], bank[6 + b % 2][:, :], ACT.Copy).then_inc(a_xTc, 1)

            def attend_k(b):
                act.wait_ge(a_q, b + 1)
                if b >= 2:
                    act.wait_ge(a_y, b - 1)
                bq = bias_cols[:, E * CH:E * CH + 1]
                s.activation(q32[:, b % 2, :], bank[0][:, :], ACT.Identity, bias=bq).then_inc(a_qe, 1)
                s.activation(q_sq[:, b % 2, :], bank[0][:, :], ACT.Square, bias=bq).then_inc(a_qe, 1)
                act.wait_ge(a_kv, 2 * b + 2)
                if b:
                    act.wait_ge(a_kk, b)
                col = 2 * NT + b * TB
                for t in range(TB):
                    r = s.activation(k_sq[:, t, :], kv[:, t, 0:D], ACT.Square, accum_out=sq[:, col + t:col + t + 1])
                r.then_inc(a_kk, 1)
                act.wait_ge(a_kk, b + 1)
                s.activation(root[:, col:col + TB], sq[:, col:col + TB], ACT.Sqrt).then_inc(a_rk, 1)

            def attend_q(b):
                act.wait_ge(a_sum, b + 1)
                col = 3 * NT + b * TB
                s.activation(root[:, col:col + TB], bank[3][:, 0:TB], ACT.Sqrt).then_inc(a_rq, 1)

            for b in range(BB):
                route_root(b)
            for b in range(BB):
                route_front(0, b)
            act.wait_ge(bias_T, 1)
            s.activation(bias_cols[:, :], bank[5][:, 0:E * CH + 1], ACT.Copy).then_inc(bias_ok, 1)
            act.wait_ge(bias_ok, 1)
            for e in range(E):
                split_weights(e)
            route_exp(0)
            experts(0)
            for i in range(BATCH + 3):
                if i < BATCH:
                    attend_a(i)
                if 0 <= i - 1 < BATCH:
                    attend_k(i - 1)
                if i >= 3:
                    route_root(i - 3)
                    route_front(1, i - 3)
                if 0 <= i - 2 < BATCH:
                    attend_q(i - 2)
            route_exp(1)
            experts(1)

        @block.vector
        def _(dve):
            v = nc.vector
            count = [0]

            def link(ins):
                count[0] += 1
                ins.then_inc(chain, 1)
                dve.wait_ge(chain, count[0])

            roots = [0]

            def moments(src, col):
                for t in range(TB):
                    r = v.bn_stats(stats[:, col + t, :], src(t))
                link(r)
                for t in range(TB):
                    r = v.bn_aggr(mv[:, col + t, :], stats[:, col + t, :])
                link(r)
                cols = slice(col, col + TB)
                v.tensor_scalar(sq[:, cols], mv[:, cols, 1], EPS, None, ALU.add).then_inc(root_of, 1)

            def scale_and_shift(col, done):
                roots[0] += 1
                dve.wait_ge(rooted, roots[0])
                cols = slice(col, col + TB)
                link(v.reciprocal(rstd[:, cols], root[:, cols]))
                v.scalar_tensor_tensor(out=shift[:, cols], in0=mv[:, cols, 0], scalar=-1.0, in1=rstd[:, cols],
                                       op0=ALU.mult, op1=ALU.mult).then_inc(done, 1)

            def route_moments(n, b):
                if n == 0:
                    dve.wait_ge(x_in[b], 16)
                moments(lambda t: res[:, b * TB + t, :], b * TB)

            def route_low(n, b):
                k, g0 = n % NB, n * BB + b
                tt = slice(b * TB, (b + 1) * TB)
                dve.wait_ge(r_hi, g0 + 1)
                v.tensor_tensor(x_s[:, k, tt, 1, :], xn[:, tt, :], x_s[:, k, tt, 0, :], ALU.subtract).then_inc(r_lo, 1)

            def choose(n):
                k = n % NB
                pri = prio[:, :].unsqueeze(1).to_broadcast((P, NT, E))
                dve.wait_ge(r_lg, (n + 1) * BB)
                link(v.tensor_tensor(lg[:, :, :], bank[4][:, 0:NT * E].rearrange("p (t e) -> p t e", e=E),
                                     b_r[:, :].unsqueeze(1).to_broadcast((P, NT, E)), ALU.add))
                for c in range(2):
                    link(v.tensor_reduce(top[:, c, :], lg[:, :, :], AX_X, ALU.max))
                    link(v.tensor_tensor(t0[:, :, :], lg[:, :, :], top[:, c, :].unsqueeze(2).to_broadcast((P, NT, E)), ALU.is_equal))
                    link(v.tensor_tensor(t1[:, :, :], t0[:, :, :], pri, ALU.mult))
                    link(v.tensor_reduce(pr[:, :], t1[:, :, :], AX_X, ALU.max))
                    link(v.tensor_tensor(oh[:, c, :, :], pri, pr[:, :].unsqueeze(2).to_broadcast((P, NT, E)), ALU.is_equal))
                    if c == 0:
                        link(v.scalar_tensor_tensor(out=lg[:, :, :], in0=oh[:, 0, :, :], scalar=FAR, in1=lg[:, :, :],
                                                    op0=ALU.mult, op1=ALU.add))
                v.tensor_tensor(mask16[:, :, :], oh[:, 0, :, :], oh[:, 1, :, :], ALU.add).then_inc(r_mask, 1)
                v.tensor_tensor(dlt[:, :], top[:, 1, :], top[:, 0, :], ALU.subtract).then_inc(r_dlt, 1)

            def weights(n):
                k = n % NB
                dve.wait_ge(r_ex, n + 1)
                link(v.tensor_scalar(den[:, :], ex[:, k, :], 1.0, None, ALU.add))
                link(v.reciprocal(den[:, :], den[:, :]))
                v.tensor_scalar(wgt[:, k, 0, :], den[:, :], 0.5, None, ALU.mult)
                link(v.scalar_tensor_tensor(out=wgt[:, k, 1, :], in0=den[:, :], scalar=0.5, in1=ex[:, k, :],
                                            op0=ALU.mult, op1=ALU.mult))

            def place(n):
                k = n % NB
                dve.wait_ge(r_pre, n + 1)
                link(v.tensor_scalar(cnt_i[:, :], bank[4][:, 256:256 + E], float(P - 1), None, ALU.add))
                link(v.tensor_scalar(til_i[:, :], cnt_i[:, :], 7, None, ALU.arith_shift_right))
                link(v.tensor_copy(til[:, :], til_i[:, :]))
                link(v.tensor_tensor(t2[:, :, :], before_e[:, :, :], til[:, :].unsqueeze(1).to_broadcast((P, E, E)), ALU.mult))
                link(v.tensor_reduce(start[:, :], t2[:, :, :], AX_X, ALU.add))
                link(v.scalar_tensor_tensor(out=base[:, :, :], in0=start[:, :].unsqueeze(1).to_broadcast((P, NT, E)), scalar=float(P),
                                            in1=bank[5][:, 0:NT * E].rearrange("p (t e) -> p t e", e=E),
                                            op0=ALU.mult, op1=ALU.add))
                for c, t in ((0, t0), (1, t1)):
                    link(v.tensor_tensor(t[:, :, :], oh[:, c, :, :], base[:, :, :], ALU.mult))
                    link(v.tensor_reduce(slot[:, :, c], t[:, :, :], AX_X, ALU.add))
                link(v.tensor_copy(slot_i[:, k, :, :], slot[:, :, :]))
                flat = slot_i[:, k, :, :].rearrange("p t c -> p (t c)")
                v.tensor_scalar(sp_i[:, 0, :], flat, 7, None, ALU.arith_shift_right)
                link(v.tensor_scalar(sp_i[:, 1, :], flat, P - 1, None, ALU.bitwise_and))
                link(v.tensor_copy(sp_f[:, :, :], sp_i[:, :, :]))
                I = 2 * NT
                if n:
                    dve.wait_ge(r_ids, n)
                for i in range(I):
                    r = v.tensor_scalar(pos_oh[:, i, :], iota16[:, :], sp_f[:, 1, i:i + 1], None, ALU.is_equal)
                r.then_inc(r_oh, 1)
                v.tensor_tensor(tile_oh[:, :, :], iota_tile[:, :].unsqueeze(1).to_broadcast((P, I, SLOT_TILES)),
                                     sp_f[:, 0, :].unsqueeze(2).to_broadcast((P, I, SLOT_TILES)), ALU.is_equal).then_inc(r_toh, 1)
                dve.wait_ge(r_toh, n + 1)
                v.tensor_tensor(tile_id[:, :, 0, :], tile_oh[:, :, :],
                                tok_id[:, :, :].rearrange("p t c -> p (t c)").unsqueeze(2).to_broadcast((P, I, SLOT_TILES)),
                                ALU.mult).then_inc(r_oh, 1)
                link(v.tensor_tensor(t3[:, :, :], iota_tile[:, :].unsqueeze(2).to_broadcast((P, SLOT_TILES, E)),
                                     start[:, :].unsqueeze(1).to_broadcast((P, SLOT_TILES, E)), ALU.is_ge))
                link(v.tensor_reduce(eid_f[:, :], t3[:, :, :], AX_X, ALU.add))
                v.tensor_scalar(eid[:, k, :], eid_f[:, :], -1.0, None, ALU.add).then_inc(r_eid, 1)
                dve.wait_ge(r_ids, n + 1)
                link(v.tensor_copy(ids_f[:, :], bank[5][:, 256:256 + SLOT_TILES]))
                link(v.scalar_tensor_tensor(out=dest_f[:, :], in0=bank[5][:, 256 + SLOT_TILES:256 + 2 * SLOT_TILES],
                                            scalar=float(BLOCK), in1=ids_f[:, :], op0=ALU.mult, op1=ALU.add))
                v.tensor_scalar(dest[:, k, :], dest_f[:, :], 2.0 * BLOCK, None, ALU.add)
                v.tensor_copy(ids[:, k, :], ids_f[:, :]).then_inc(r_idc, 1)

            def split_hidden(q):
                dve.wait_ge(f_hid, q + 1)
                if q >= 2:
                    dve.wait_ge(f_m2, q - 1)
                link(v.tensor_copy(h_s[:, q % 2, 0, :], hid[:, q % 2, :]))
                v.tensor_tensor(h_s[:, q % 2, 1, :], hid[:, q % 2, :], h_s[:, q % 2, 0, :], ALU.subtract).then_inc(f_hs, 1)

            def expert_out(q, e):
                dve.wait_ge(f_m2, q + 1)
                if q >= 2:
                    dve.wait_ge(f_y, q - 1)
                ps = bank[2 + q % 2]
                link(v.scalar_tensor_tensor(out=y_lo[:, q % 2, :], in0=ps[:, D:2 * D], scalar=1.0 / W_SCALE,
                                            in1=b_2[:, bass.ds(e, 1), :].rearrange("p a d -> p (a d)"),
                                            op0=ALU.mult, op1=ALU.add))
                if q >= NY:
                    dve.wait_ge(f_st[q % NY], 16 * (q // NY))
                v.scalar_tensor_tensor(out=y_sb[:, q % NY, :], in0=ps[:, 0:D], scalar=1.0 / W_SCALE, in1=y_lo[:, q % 2, :],
                                       op0=ALU.mult, op1=ALU.add).then_inc(f_y, 1)

            def experts(n):
                split_hidden(n * SLOT_TILES)
                for j in range(SLOT_TILES):
                    q = n * SLOT_TILES + j
                    if j + 1 < SLOT_TILES:
                        split_hidden(q + 1)
                    if j % LOAD == 0:
                        e_of = load_experts(mybir.EngineType.DVE, n, j)
                    expert_out(q, e_of[j % LOAD])

            def combine(n, b):
                k = n % NB
                dve.wait_ge(c_got[b], 16 * (n + 1))
                for c in range(2):
                    for t in range(TB):
                        i = b * TB + t
                        r = v.scalar_tensor_tensor(out=(part, res)[c][:, i, :], in0=back[:, b, c, t, :], scalar=wgt[:, k, c, i:i + 1],
                                                   in1=(res, part)[c][:, i, :], op0=ALU.mult, op1=ALU.add)
                    if c == 0:
                        link(r)
                r.then_inc(c_done, 1)
                dve.wait_ge(c_done, n * BB + b + 1)

            def attend_a(b):
                combine(0, b)
                moments(lambda t: res[:, b * TB + t, :], NT + b * TB)
                v.tensor_tensor(res_b[:, b, :, :], res[:, b * TB:(b + 1) * TB, :],
                                b_o[:, :].unsqueeze(1).to_broadcast((P, TB, D)), ALU.add).then_inc(a_rb, 1)
                scale_and_shift(NT + b * TB, a_s)

            def attend_k(b):
                dve.wait_ge(a_kvm, b + 1)
                if b:
                    dve.wait_ge(a_kk, b)
                for h in range(2):
                    v.tensor_tensor(kv[:, 2 * h:2 * h + 2, :], bank[1 + h][:, :].rearrange("p (t n) -> p t n", t=2),
                                    b_kv[:, :].unsqueeze(1).to_broadcast((P, 2, 2 * D)), ALU.add).then_inc(a_kv, 1)
                dve.wait_ge(a_kv, 2 * b + 2)
                if b >= 2:
                    dve.wait_ge(a_sum, b - 1)
                link(v.tensor_tensor(kxv[:, b % 2, :, :], kv[:, :, 0:D], kv[:, :, D:2 * D], ALU.mult))
                dve.wait_ge(a_rk, b + 1)
                col = 2 * NT + b * TB
                v.reciprocal(rstd[:, col:col + TB], root[:, col:col + TB]).then_inc(a_p, 1)

            def attend_q(b):
                dve.wait_ge(a_rq, b + 1)
                col = 3 * NT + b * TB
                v.tensor_copy(kv_sum[:, :], bank[3][:, 64:65]).then_inc(chain, 1)
                count[0] += 1
                v.reciprocal(rstd[:, col:col + TB], root[:, col:col + TB])
                dve.wait_ge(chain, count[0])
                if b:
                    dve.wait_ge(a_y, b)
                v.tensor_scalar(wout_b[:, :], wout[:, :], kv_sum[:, 0:1], None, ALU.mult).then_inc(a_w, 1)
                dve.wait_ge(a_w, b + 1)

            def attend_r(b):
                col = 3 * NT + b * TB
                dve.wait_ge(a_rb, b + 1)
                dve.wait_ge(a_y, b + 1)
                for t in range(TB):
                    r = v.scalar_tensor_tensor(out=res[:, b * TB + t, :], in0=bank[5][:, t * D:(t + 1) * D],
                                               scalar=rstd[:, col + t:col + t + 1], in1=res_b[:, b, t, :], op0=ALU.mult, op1=ALU.add)
                r.then_inc(a_res, 1)
                dve.wait_ge(a_res, b + 1)

            def split_w1(e):
                dve.wait_ge(w1_hi, e + 1)
                v.scalar_tensor_tensor(out=w1_s[:, e, 1, :], in0=w1_raw[:, e, :], scalar=W_SCALE,
                                       in1=w1_s[:, e, 0, :], op0=ALU.mult, op1=ALU.subtract).then_inc(w1_lo, 1)

            dve.wait_ge(consts, 14)
            dve.wait_ge(small_in, 32)
            for b in range(BB):
                route_moments(0, b)
            for b in range(BB):
                scale_and_shift(b * TB, r_s)
            for b in range(BB):
                route_low(0, b)
            choose(0)
            place(0)
            weights(0)
            for e in range(E):
                split_w1(e)
            dve.wait_ge(bias_in, 16 * 7)
            experts(0)

            for i in range(BATCH + 3):
                if i < BATCH:
                    attend_a(i)
                if 0 <= i - 1 < BATCH:
                    attend_k(i - 1)
                if i >= 3:
                    attend_r(i - 3)
                    route_moments(1, i - 3)
                    scale_and_shift((i - 3) * TB, r_s)
                    route_low(1, i - 3)
                if 0 <= i - 2 < BATCH:
                    attend_q(i - 2)
            choose(1)
            place(1)
            weights(1)
            experts(1)
            for b in range(BB):
                combine(1, b)

        @block.tensor
        def _(pe):
            mm = nc.tensor.matmul

            def route_turn(n, b):
                g0 = n * BB + b
                pe.wait_ge(r_xn, g0 + 1)
                if g0 >= 2:
                    pe.wait_ge(r_xT, g0 - 1)
                for t in range(TB):
                    r = nc.tensor.transpose(bank[6 + b % 2][:, t * P:(t + 1) * P], xn[:, b * TB + t, :], ident[:, :])
                r.then_inc(r_T, 1)

            def route_logits(n, b):
                pe.wait_ge(r_xT, n * BB + b + 1)
                for t in range(b * TB, (b + 1) * TB):
                    r = mm(bank[4][:, t * E:(t + 1) * E], xnT[:, t * P:(t + 1) * P], wr[:, :], start=True, stop=True)
                r.then_inc(r_lg, 1)

            def route_place(n):
                pe.wait_ge(r_mask, n + 1)
                m = mask16[:, :, :].rearrange("p t e -> p (t e)")
                mm(bank[5][:, 0:NT * E], before16[:, :], m, start=True, stop=False, skip_group_check=True)
                for s in range(1, NT):
                    mm(bank[5][:, s * E:NT * E], ones16[:, :], m[:, 0:(NT - s) * E], start=False, stop=(s == NT - 1), skip_group_check=True)
                for t in range(NT):
                    r = mm(bank[4][:, 256:256 + E], ones16[:, :], m[:, t * E:(t + 1) * E], start=(t == 0), stop=(t == NT - 1))
                r.then_inc(r_pre, 1)
                pe.wait_ge(r_oh, 3 * (n + 1))
                for i in range(2 * NT):
                    r = mm(bank[5][:, 256:256 + 2 * SLOT_TILES], pos_oh[:, i, :], tile_id[:, i, :, :].rearrange("p h s -> p (h s)"), start=(i == 0), stop=(i == 2 * NT - 1))
                r.then_inc(r_ids, 1)

            def tokens_T(q):
                pe.wait_ge(f_got[q % NG], 16 * (q // NG + 1))
                for h in range(2):
                    r = nc.tensor.transpose(bank16(4 + q % 2)[:, h * D:(h + 1) * D], got[:, q % NG, h * D:(h + 1) * D], ident16[:, :])
                r.then_inc(f_T, 1)

            def product1(q, e):
                pe.wait_ge(f_xT, q + 1)
                x_hi, x_lo = xT[:, q % 2, 0:D], xT[:, q % 2, D:2 * D]
                for c in range(CH):
                    o = bank[q % 2][:, c * P:(c + 1) * P]
                    w = [w1_s[:, bass.ds(e, 1), h, c * P:(c + 1) * P].rearrange("p a f -> p (a f)") for h in range(2)]
                    mm(o, w[0], x_hi, start=True, stop=False)
                    mm(o, w[0], x_lo, start=False, stop=False)
                    r = mm(o, w[1], x_hi, start=False, stop=True)
                r.then_inc(f_m1, 1)

            def product2(q, e):
                pe.wait_ge(f_hs, q + 1)
                o = bank[2 + q % 2]
                for c in range(CH):
                    w = w2_s[:, bass.ds(e, 1), c, :, :].rearrange("p a h d -> p (a h d)")
                    mm(o[:, 0:2 * D], h_s[:, q % 2, 0, c * P:(c + 1) * P], w, start=(c == 0), stop=False, skip_group_check=True)
                    r = mm(o[:, 0:D], h_s[:, q % 2, 1, c * P:(c + 1) * P], w[:, 0:D], start=False, stop=(c == CH - 1), skip_group_check=True)
                r.then_inc(f_m2, 1)

            def experts(n):
                q0, k = n * SLOT_TILES, n % NB
                pe.wait_ge(r_eid, n + 1)
                pe.wait_ge(r_idc, n + 1)
                tokens_T(q0)
                e_of = load_experts(mybir.EngineType.PE, n, 0)
                tokens_T(q0 + 1)
                product1(q0, e_of[0])
                e = e_of[0]
                for j in range(SLOT_TILES):
                    if j + 2 < SLOT_TILES:
                        tokens_T(q0 + j + 2)
                    if j + 1 < SLOT_TILES:
                        if (j + 1) % LOAD == 0:
                            after = load_experts(mybir.EngineType.PE, n, j + 1)
                        else:
                            after = e_of
                        product1(q0 + j + 1, after[(j + 1) % LOAD])
                    product2(q0 + j, e_of[j % LOAD])
                    e_of = after

            def attend_a(b):
                pe.wait_ge(a_n, b + 1)
                for t in range(TB):
                    r = nc.tensor.transpose(bank[6 + b % 2][:, t * P:(t + 1) * P], a_xn[:, b % 2, t, :], ident[:, :])
                r.then_inc(a_T, 1)

            def attend_k(b):
                pe.wait_ge(a_xTc, b + 1)
                if b:
                    pe.wait_ge(a_qe, 2 * b)
                    pe.wait_ge(a_kv, 2 * b)
                for t in range(TB):
                    r = mm(bank[1 + t // 2][:, (t % 2) * 2 * D:(t % 2 + 1) * 2 * D], a_xT[:, t * P:(t + 1) * P], wqkv[:, D:3 * D],
                           start=True, stop=True)
                r.then_inc(a_kvm, 1)
                mm(bank[0][:, :], wqkv[:, 0:D], a_xT[:, :], start=True, stop=True).then_inc(a_q, 1)

            def attend_q(b):
                pe.wait_ge(a_qe, 2 * b + 2)
                for t in range(TB):
                    mm(bank[3][:, t:t + 1], q_sq[:, b % 2, t * P:(t + 1) * P], ones[:, :], start=True, stop=True)
                pe.wait_ge(a_p, b + 1)
                col = 2 * NT + b * TB
                for t in range(TB):
                    r = mm(bank[3][:, 64:65], kxv[:, b % 2, t, :], rstd[:, col + t:col + t + 1], start=(t == 0), stop=(t == TB - 1))
                r.then_inc(a_sum, 1)
                if b:
                    pe.wait_ge(a_res, b)
                pe.wait_ge(a_w, b + 1)
                for t in range(TB):
                    r = mm(bank[5][:, t * D:(t + 1) * D], q32[:, b % 2, t * P:(t + 1) * P], wout_b[:, :], start=True, stop=True)
                r.then_inc(a_y, 1)

            pe.wait_ge(consts, 14)
            pe.wait_ge(small_in, 32)
            for b in range(BB):
                route_turn(0, b)
                if b:
                    route_logits(0, b - 1)
            route_logits(0, BB - 1)
            pe.wait_ge(bias_in, 16 * 7)
            R = E * CH + 1
            nc.tensor.transpose(bank[5][:, 0:R], bias_rows[:, :], ident[0:R, 0:R]).then_inc(bias_T, 1)
            pe.wait_ge(bias_ok, 1)
            route_place(0)
            pe.wait_ge(w1_lo, E)
            pe.wait_ge(w2_lo, E)
            experts(0)
            pe.wait_ge(f_y, SLOT_TILES)
            for i in range(BATCH + 3):
                if i < BATCH:
                    attend_a(i)
                if 0 <= i - 1 < BATCH:
                    attend_k(i - 1)
                if i >= 3:
                    route_turn(1, i - 3)
                    route_logits(1, i - 3)
                if 0 <= i - 2 < BATCH:
                    attend_q(i - 2)
            route_place(1)
            experts(1)


_INS = ['L0_attn_x', 'L0_attn_Wqkv', 'L0_attn_bqkv', 'L0_attn_Wout', 'L0_attn_bout', 'L0_ffn_W_router',
        'L0_ffn_b_router', 'L0_ffn_W1', 'L0_ffn_b1', 'L0_ffn_W2', 'L0_ffn_b2']


def kernel(**inputs):
    import numpy as _np
    import concourse.bacc as _bacc
    from concourse import mybir as _mybir
    from concourse.bass_utils import run_bass_kernel_spmd as _run

    nc = _bacc.Bacc("TRN2", target_bir_lowering=False, num_devices=1)
    arrays, args = {}, []
    for name in _INS:
        a = _np.ascontiguousarray(inputs[name])
        arrays[f"in_{name}"] = a
        args.append(nc.dram_tensor(f"in_{name}", a.shape, _mybir.dt.from_np(a.dtype), kind="ExternalInput").ap())
    args.append(nc.dram_tensor("out_0", inputs['L0_attn_x'].shape, _mybir.dt.float32, kind="ExternalOutput").ap())
    macaron(nc, *args)
    r = _run(nc, [arrays], core_ids=[0])
    return r.results[0]["out_0"]
```

```python
from contextlib import ExitStack

import concourse.bass as bass
from concourse import mybir

P = 128
F32 = mybir.dt.float32
F16 = mybir.dt.float16
I32 = mybir.dt.int32
ALU = mybir.AluOpType
ACT = mybir.ActivationFunctionType
AX_X = mybir.AxisListType.X
EPS = 1e-5
W_SCALE = 64.0
FAR = -3.0e38


def macaron(nc, x, w_qkv, b_qkv, w_out, b_out, w_router, b_router, w1, b1, w2, b2, out):
    BATCH, SEQ, D = x.shape
    E, _, FF = w1.shape
    CH = FF // P
    TB = SEQ // P
    NB = 1
    LAYERS = 2
    BB = BATCH // NB
    NT = BB * TB
    BLOCK = NT * P
    SLOT_TILES = (2 * BLOCK + E * (P - 1)) // P
    GROUP = TB * D
    NG, NY = 8, 4
    LEAD = 5
    assert D == P and BATCH % NB == 0

    x_v = x.rearrange("b (p j) d -> b p j d", j=TB)
    out_v = out.rearrange("b (p j) d -> b p j d", j=TB)
    tok_rows = [nc.dram_tensor(f"tok_rows{k}", (BLOCK, 2 * D), F16, kind="Internal").ap() for k in range(NB)]
    pair_rows = [nc.dram_tensor(f"pair_rows{k}", (2 * BLOCK, D), F32, kind="Internal").ap() for k in range(NB)]

    with ExitStack() as ctx:
        def sb(name, shape, dt=F32):
            return ctx.enter_context(nc.sbuf_tensor(name, shape, dt))

        def sem(name):
            return ctx.enter_context(nc.semaphore(name))

        bank = [ctx.enter_context(nc.psum_tensor(f"bank{i}", [P, 512], F32)) for i in range(8)]
        def bank16(i):
            return bank[i][:, :].bitcast(F16)

        res = sb("res", [P, BATCH * TB, D])
        ident = sb("ident", [P, P])
        ident16 = sb("ident16", [P, P], F16)
        before16 = sb("before16", [P, P], F16)
        ones16 = sb("ones16", [P, P], F16)
        ones = sb("ones", [P, 1])
        iota_pos = sb("iota_pos", [P, P])
        iota_tile = sb("iota_tile", [P, SLOT_TILES])
        iota16 = sb("iota16", [P, P], F16)
        prio = sb("prio", [P, E])
        tok_id = sb("tok_id", [P, NT, 2])
        choice = sb("choice", [P, NT, 2])
        before_e = sb("before_e", [P, E, E])
        w1_raw = sb("w1_raw", [P, E, FF])
        w2_raw = sb("w2_raw", [P, E, CH, D])
        w1_s = sb("w1_s", [P, E, 2, FF], F16)
        w2_s = sb("w2_s", [P, E, CH, 2, D], F16)
        wr = sb("wr", [P, E])
        wqkv = sb("wqkv", [P, 3 * D])
        wout = sb("wout", [P, D])
        bias_rows = sb("bias_rows", [E * CH + 1, P])
        bias_cols = sb("bias_cols", [P, E * CH + 1])
        b_kv = sb("b_kv", [P, 2 * D])
        b_o = sb("b_o", [P, D])
        b_r = sb("b_r", [P, E])
        b_2 = sb("b_2", [P, E, D])
        stats = sb("stats", [P, 2 * NT, 6])
        mv = sb("mv", [P, 2 * NT, 2])
        rstd = sb("rstd", [P, 4 * NT])
        shift = sb("shift", [P, 2 * NT])
        sq = sb("sq", [P, 4 * NT])
        root = sb("root", [P, 4 * NT])
        xn = sb("xn", [P, NT, D])
        x_s = sb("x_s", [P, NB, NT, 2, D], F16)
        xnT = sb("xnT", [P, NT * P])
        lg = sb("lg", [P, NT, E])
        t0 = sb("t0", [P, NT, E])
        t1 = sb("t1", [P, NT, E])
        top = sb("top", [P, 2, NT])
        pr = sb("pr", [P, NT])
        oh = sb("oh", [P, 2, NT, E])
        mask16 = sb("mask16", [P, NT, E], F16)
        dlt = sb("dlt", [P, NT])
        ex = sb("ex", [P, NB, NT])
        den = sb("den", [P, NT])
        wgt = sb("wgt", [P, NB, 2, NT])
        cnt = sb("cnt", [P, E])
        cnt_i = sb("cnt_i", [P, E], I32)
        til_i = sb("til_i", [P, E], I32)
        til = sb("til", [P, E])
        t2 = sb("t2", [P, E, E])
        start = sb("start", [P, E])
        base = sb("base", [P, NT, E])
        slot = sb("slot", [P, NT, 2])
        slot_i = sb("slot_i", [P, NB, NT, 2], I32)
        sp_i = sb("sp_i", [P, 2, NT * 2], I32)
        sp_f = sb("sp_f", [P, 2, NT * 2])
        t3 = sb("t3", [P, SLOT_TILES, E])
        eid_f = sb("eid_f", [P, SLOT_TILES])
        eid = sb("eid", [P, NB, SLOT_TILES], I32)
        tile_oh = sb("tile_oh", [P, NT * 2, SLOT_TILES], F16)
        tile_id = sb("tile_id", [P, NT * 2, 2, SLOT_TILES], F16)
        pos_oh = sb("pos_oh", [P, NT * 2, P], F16)
        ids = sb("ids", [P, NB, SLOT_TILES], I32)
        ids_f = sb("ids_f", [P, SLOT_TILES])
        dest_f = sb("dest_f", [P, SLOT_TILES])
        dest = sb("dest", [P, NB, SLOT_TILES], I32)
        got = sb("got", [P, NG, 2 * D], F16)
        xT = sb("xT", [P, 2, 2 * D], F16)
        hid = sb("hid", [P, 2, FF])
        h_s = sb("h_s", [P, 2, 2, FF], F16)
        y_lo = sb("y_lo", [P, 2, D])
        y_sb = sb("y_sb", [P, NY, D])
        back = sb("back", [P, BB, 2, TB, D])
        part = sb("part", [P, NT, D])
        assert E * FF >= 2 * BATCH * GROUP and E * CH * D >= 2 * BATCH * GROUP
        w1_room = w1_raw[:, :, :].rearrange("p e f -> p (e f)")
        w2_room = w2_raw[:, :, :, :].rearrange("p e c d -> p (e c d)")
        A = BATCH * GROUP
        a_xn = w1_room[:, 0:A].rearrange("p (b t d) -> p b t d", b=BATCH, t=TB)
        a_xT = w1_room[:, A:2 * A].rearrange("p (b n) -> p b n", b=BATCH)
        q32 = w2_room[:, 0:A].rearrange("p (b n) -> p b n", b=BATCH)
        q_sq = w2_room[:, A:2 * A].rearrange("p (b n) -> p b n", b=BATCH)
        kv = sb("kv", [P, 2, TB, 2 * D])
        k_sq = sb("k_sq", [P, BATCH, TB, D])
        kxv = sb("kxv", [P, BATCH, TB, D])
        kv_sum = sb("kv_sum", [P, BATCH])
        wout_b = sb("wout_b", [P, BATCH, D])
        res_b = sb("res_b", [P, BATCH, TB, D])

        x_in = [sem(f"x_in{b}") for b in range(BATCH)]
        small_in = sem("small_in")
        bias_in = sem("bias_in")
        w1_in = [sem(f"w1_in{e}") for e in range(E)]
        w2_in = [sem(f"w2_in{e}") for e in range(E)]
        consts = sem("consts")
        w1_hi = sem("w1_hi")
        w1_lo = sem("w1_lo")
        w2_scaled = sem("w2_scaled")
        w2_hi = sem("w2_hi")
        w2_lo = sem("w2_lo")
        bias_T = sem("bias_T")
        bias_ok = sem("bias_ok")
        r_xn = sem("r_xn")
        r_hi = sem("r_hi")
        r_lo = sem("r_lo")
        r_store = [sem(f"r_store{k}") for k in range(NB)]
        r_T = sem("r_T")
        r_xT = sem("r_xT")
        r_lg = sem("r_lg")
        r_lgc = sem("r_lgc")
        r_mask = sem("r_mask")
        r_pre = sem("r_pre")
        r_pred = sem("r_pred")
        r_toh = sem("r_toh")
        r_dlt = sem("r_dlt")
        r_ex = sem("r_ex")
        r_oh = sem("r_oh")
        r_ids = sem("r_ids")
        r_idc = sem("r_idc")
        r_eid = sem("r_eid")
        f_got = [sem(f"f_got{i}") for i in range(NG)]
        f_T = sem("f_T")
        f_xT = sem("f_xT")
        f_m1 = sem("f_m1")
        f_hid = sem("f_hid")
        f_hs = sem("f_hs")
        f_m2 = sem("f_m2")
        f_y = sem("f_y")
        f_st = [sem(f"f_st{i}") for i in range(NY)]
        c_got = [sem(f"c_got{b}") for b in range(BB)]
        c_done = sem("c_done")
        a_s = sem("a_s")
        r_s = sem("r_s")
        a_n = sem("a_n")
        a_T = sem("a_T")
        a_xTc = sem("a_xTc")
        a_q = sem("a_q")
        a_qe = sem("a_qe")
        a_kvm = sem("a_kvm")
        a_kv = sem("a_kv")
        a_p = sem("a_p")
        a_ss = sem("a_ss")
        a_sum = sem("a_sum")
        a_w = sem("a_w")
        a_y = sem("a_y")
        a_res = sem("a_res")
        a_rk = sem("a_rk")
        a_kxv = sem("a_kxv")
        a_rq = sem("a_rq")
        a_rb = sem("a_rb")
        a_var = sem("a_var")
        a_dev = sem("a_dev")
        r_var = sem("r_var")
        r_dev = sem("r_dev")
        chain = sem("chain")
        a_kk = sem("a_kk")
        out_st = sem("out_st")


        def stored_all(eng, n):
            done = (n + 1) * SLOT_TILES
            for i in range(NY):
                eng.wait_ge(f_st[i], 16 * ((done - i + NY - 1) // NY))

        def slots(order):
            for i in range(BATCH + 5):
                for stage, late in order:
                    if 0 <= i - late < BATCH:
                        stage(i - late)

        LOAD = 8

        def load_experts(engine, n, j):
            return nc.values_load_multi_w_load_instructions(
                eid[0:1, n % NB, j:min(j + LOAD, SLOT_TILES)], engines=(engine,), min_val=0, max_val=E - 1,
                skip_runtime_bounds_check_because="an expert is a count of at most E starts, less one")[1]

        block = ctx.enter_context(nc.Block())

        @block.sync
        def _(sp):
            for b in range(BATCH):
                sp.dma_start(res[:, b * TB:(b + 1) * TB, :], x_v[b]).then_inc(x_in[b], 16)
                if b == 0:
                    sp.dma_start(wr[:, :], w_router).then_inc(small_in, 16)
                    sp.dma_start(b_r[:, :], b_router.rearrange("(a n) -> a n", a=1).to_broadcast((P, E))).then_inc(small_in, 16)
            for e in range(E):
                sp.dma_start(w1_raw[:, e, :], w1[e]).then_inc(w1_in[e], 16)

            def store_tokens(n):
                k = n % NB
                for b in range(BB):
                    sp.wait_ge(r_lo, n * BB + b + 1)
                    sp.dma_start(tok_rows[k].rearrange("(b p j) d -> b p (j d)", b=BB, j=TB)[b],
                                 x_s[:, k, b * TB:(b + 1) * TB, :, :].rearrange("p t h d -> p (t h d)")).then_inc(r_store[k], 16)

            def fetch_pairs(n):
                k = n % NB
                stored_all(sp, n)
                rows = pair_rows[k].rearrange("(c b p j) d -> b p c (j d)", c=2, b=BB, j=TB)
                for b in range(BB):
                    if n >= NB:
                        sp.wait_ge(c_done, (n - NB) * BB + b + 1)
                    sp.dma_start(back[:, b, :, :, :].rearrange("p c j d -> p c (j d)"), rows[b]).then_inc(c_got[b], 16)

            for n in range(LAYERS * NB):
                store_tokens(n)
                fetch_pairs(n)
            for b in range(BATCH):
                sp.wait_ge(c_done, (LAYERS - 1) * BATCH + b + 1)
                sp.dma_start(out_v[b], res[:, b * TB:(b + 1) * TB, :]).then_inc(out_st, 16)
            sp.wait_ge(out_st, 16 * BATCH)

        @block.gpsimd
        def _(pool):
            g = nc.gpsimd
            g.memset(ident[:, :], 0.0).then_inc(consts, 1)
            g.memset(ones16[:, :], 1.0).then_inc(consts, 1)
            g.memset(ones[:, :], 1.0).then_inc(consts, 1)
            g.memset(t2[:, :, :], 1.0).then_inc(consts, 1)
            pool.wait_ge(consts, 4)
            g.affine_select(out=ident[:, :], in_=ident[:, :], compare_op=ALU.not_equal, fill=1.0, base=0,
                            pattern=[[-1, P]], channel_multiplier=1).then_inc(consts, 1)
            pool.wait_ge(consts, 5)
            g.tensor_copy(ident16[:, :], ident[:, :]).then_inc(consts, 1)
            g.affine_select(out=before16[:, :], in_=ones16[:, :], compare_op=ALU.is_gt, fill=0.0, base=0,
                            pattern=[[1, P]], channel_multiplier=-1).then_inc(consts, 1)
            g.affine_select(out=before_e[:, :, :], in_=t2[:, :, :], compare_op=ALU.is_gt, fill=0.0, base=0,
                            pattern=[[1, E], [-1, E]], channel_multiplier=0).then_inc(consts, 1)
            g.iota(iota_pos[:, :], [[1, P]], base=0, channel_multiplier=0,
                   allow_small_or_imprecise_dtypes=True).then_inc(consts, 1)
            g.iota(iota_tile[:, :], [[1, SLOT_TILES]], base=0, channel_multiplier=0,
                   allow_small_or_imprecise_dtypes=True).then_inc(consts, 1)
            g.iota(prio[:, :], [[-1, E]], base=E, channel_multiplier=0,
                   allow_small_or_imprecise_dtypes=True).then_inc(consts, 1)
            g.iota(tok_id[:, :, :], [[SEQ, BB], [1, TB], [0, 2]], base=0, channel_multiplier=TB,
                   allow_small_or_imprecise_dtypes=True).then_inc(consts, 1)
            g.iota(choice[:, :, :], [[0, NT], [1, 2]], base=-2, channel_multiplier=0,
                   allow_small_or_imprecise_dtypes=True).then_inc(consts, 1)
            pool.wait_ge(consts, 13)
            g.tensor_copy(iota16[:, :], iota_pos[:, :]).then_inc(consts, 1)
            for e in range(E):
                pool.wait_ge(w2_in[e], 16)
                g.tensor_scalar(w2_raw[:, e, :, :], w2_raw[:, e, :, :], W_SCALE, None, ALU.mult).then_inc(w2_scaled, 1)
            for e in range(E):
                pool.wait_ge(w2_scaled, e + 1)
                pool.wait_ge(w2_hi, e + 1)
                g.tensor_tensor(w2_s[:, e, :, 1, :], w2_raw[:, e, :, :], w2_s[:, e, :, 0, :], ALU.subtract).then_inc(w2_lo, 1)

            def dispatch(n, j):
                k, q = n % NB, n * SLOT_TILES + j
                if j == 0:
                    pool.wait_ge(r_idc, n + 1)
                    pool.wait_ge(r_store[k], 16 * BB * (n // NB + 1))
                if q >= NG:
                    pool.wait_ge(f_T, q - NG + 1)
                g.indirect_dma_start(got[:, q % NG, :], None, tok_rows[k],
                                     bass.IndirectOffsetOnAxis(ap=ids[:, k, j:j + 1], axis=0)).then_inc(f_got[q % NG], 16)

            def give_back(n, j):
                k, q = n % NB, n * SLOT_TILES + j
                pool.wait_ge(f_y, q + 1)
                g.indirect_dma_start(pair_rows[k], bass.IndirectOffsetOnAxis(ap=dest[:, k, j:j + 1], axis=0), y_sb[:, q % NY, :],
                                     None, bounds_check=2 * BLOCK - 1, oob_is_err=False).then_inc(f_st[q % NY], 16)

            for n in range(LAYERS * NB):
                pool.wait_ge(r_toh, n + 1)
                g.tensor_tensor(tile_id[:, :, 1, :], tile_oh[:, :, :],
                                choice[:, :, :].rearrange("p t c -> p (t c)").unsqueeze(2).to_broadcast((P, 2 * NT, SLOT_TILES)),
                                ALU.mult).then_inc(r_oh, 1)
                for j in range(SLOT_TILES + LEAD):
                    if j < SLOT_TILES:
                        dispatch(n, j)
                    if j >= LEAD:
                        give_back(n, j - LEAD)

        @block.scalar
        def _(act):
            s = nc.scalar
            act.dma_start(bias_rows[0:E * CH, :], b1.rearrange("e (c p) -> (e c) p", p=P)).then_inc(bias_in, 16)
            act.dma_start(bias_rows[E * CH:E * CH + 1, :], b_qkv[0:D].rearrange("(a n) -> a n", a=1)).then_inc(bias_in, 16)
            act.dma_start(wqkv[:, :], w_qkv).then_inc(bias_in, 16)
            act.dma_start(wout[:, :], w_out).then_inc(bias_in, 16)
            act.dma_start(b_kv[:, :], b_qkv[D:3 * D].rearrange("(a n) -> a n", a=1).to_broadcast((P, 2 * D))).then_inc(bias_in, 16)
            act.dma_start(b_o[:, :], b_out.rearrange("(a n) -> a n", a=1).to_broadcast((P, D))).then_inc(bias_in, 16)
            act.dma_start(b_2[:, :, :].rearrange("p e d -> p (e d)"),
                          b2.rearrange("(a e) d -> a (e d)", a=1).to_broadcast((P, E * D))).then_inc(bias_in, 16)
            for e in range(E):
                act.dma_start(w2_raw[:, e, :, :], w2[e].rearrange("(c p) d -> p c d", p=P)).then_inc(w2_in[e], 16)

            def split_weights(e):
                act.wait_ge(w1_in[e], 16)
                s.activation(w1_s[:, e, 0, :], w1_raw[:, e, :], ACT.Copy, scale=W_SCALE).then_inc(w1_hi, 1)
                act.wait_ge(w2_scaled, e + 1)
                s.activation(w2_s[:, e, :, 0, :], w2_raw[:, e, :, :], ACT.Copy).then_inc(w2_hi, 1)

            def root_act(col, asked, waited, done):
                act.wait_ge(asked, waited)
                s.activation(root[:, col:col + TB], sq[:, col:col + TB], ACT.Sqrt).then_inc(done, 1)

            def normalise(src, dst, col, ready, waited, done):
                act.wait_ge(ready, waited)
                for t in range(TB):
                    r = s.activation(dst(t), src(t), ACT.Identity, scale=rstd[:, col + t:col + t + 1], bias=shift[:, col + t:col + t + 1])
                r.then_inc(done, 1)

            def route_root(n, b):
                root_act(b * TB, r_var, n * BB + b + 1, r_dev)

            def route_front(n, b):
                k, g0 = n % NB, n * BB + b
                tt = slice(b * TB, (b + 1) * TB)
                if n:
                    act.wait_ge(r_T, (n - 1) * BB + b + 1)
                    act.wait_ge(r_lo, (n - 1) * BB + b + 1)
                normalise(lambda t: res[:, b * TB + t, :], lambda t: xn[:, b * TB + t, :], b * TB, r_s, g0 + 1, r_xn)
                act.wait_ge(r_xn, g0 + 1)
                if n >= NB:
                    act.wait_ge(r_store[k], 16 * BB * (n // NB))
                s.activation(x_s[:, k, tt, 0, :], xn[:, tt, :], ACT.Copy).then_inc(r_hi, 1)
                act.wait_ge(r_T, g0 + 1)
                if n:
                    act.wait_ge(r_lg, (n - 1) * BB + b + 1)
                s.activation(xnT[:, b * GROUP:(b + 1) * GROUP], bank[7][:, :], ACT.Copy).then_inc(r_xT, 1)

            def route_exp(n):
                act.wait_ge(r_dlt, n + 1)
                s.activation(ex[:, n % NB, :], dlt[:, :], ACT.Exp).then_inc(r_ex, 1)

            def tokens_T(q):
                act.wait_ge(f_T, q + 1)
                if q >= 2:
                    act.wait_ge(f_m1, q - 1)
                s.activation(xT[:, q % 2, :], bank16(4 + q % 2)[:, 0:2 * D], ACT.Copy).then_inc(f_xT, 1)

            def hidden(q, e):
                act.wait_ge(f_m1, q + 1)
                if q >= 2:
                    act.wait_ge(f_hs, q - 1)
                for c in range(CH):
                    r = s.activation(hid[:, q % 2, c * P:(c + 1) * P], bank[q % 2][:, c * P:(c + 1) * P], ACT.Relu,
                                     bias=bias_cols[:, bass.ds(e * CH + c, 1)], scale=1.0 / W_SCALE)
                r.then_inc(f_hid, 1)

            def experts(n):
                act.wait_ge(r_eid, n + 1)
                tokens_T(n * SLOT_TILES)
                for j in range(SLOT_TILES):
                    q = n * SLOT_TILES + j
                    if j + 1 < SLOT_TILES:
                        tokens_T(q + 1)
                    if j % LOAD == 0:
                        e_of = load_experts(mybir.EngineType.Activation, n, j)
                    hidden(q, e_of[j % LOAD])

            def attend_root(b):
                root_act(NT + b * TB, a_var, b + 1, a_dev)

            def attend_norm(b):
                normalise(lambda t: res[:, b * TB + t, :], lambda t: a_xn[:, b, t, :], NT + b * TB, a_s, b + 1, a_n)
                act.wait_ge(a_T, b + 1)
                s.activation(a_xT[:, b, :], bank[6][:, :], ACT.Copy).then_inc(a_xTc, 1)

            def attend_keys(b):
                act.wait_ge(a_q, b + 1)
                bq = bias_cols[:, E * CH:E * CH + 1]
                s.activation(q32[:, b, :], bank[0][:, :], ACT.Identity, bias=bq).then_inc(a_qe, 1)
                s.activation(q_sq[:, b, :], bank[0][:, :], ACT.Square, bias=bq).then_inc(a_qe, 1)
                act.wait_ge(a_kv, 2 * b + 2)
                col = 2 * NT + b * TB
                for t in range(TB):
                    r = s.activation(k_sq[:, b, t, :], kv[:, b % 2, t, 0:D], ACT.Square, accum_out=sq[:, col + t:col + t + 1])
                r.then_inc(a_kk, 1)
                act.wait_ge(a_kk, b + 1)
                s.activation(root[:, col:col + TB], sq[:, col:col + TB], ACT.Sqrt).then_inc(a_rk, 1)

            def attend_sum(b):
                act.wait_ge(a_sum, b + 1)
                col = 3 * NT + b * TB
                s.activation(root[:, col:col + TB], bank[3][:, 0:TB], ACT.Sqrt).then_inc(a_rq, 1)

            for b in range(BB):
                route_root(0, b)
            for b in range(BB):
                route_front(0, b)
            act.wait_ge(bias_T, 1)
            s.activation(bias_cols[:, :], bank[5][:, 0:E * CH + 1], ACT.Copy).then_inc(bias_ok, 1)
            act.wait_ge(bias_ok, 1)
            for e in range(E):
                split_weights(e)
            route_exp(0)
            experts(0)
            act.wait_ge(w1_lo, E)
            act.wait_ge(w2_lo, E)
            slots([(attend_sum, 3), (attend_norm, 1), (attend_keys, 2), (lambda b: route_front(1, b), 5),
                   (attend_root, 0), (lambda b: route_root(1, b), 4)])
            route_exp(1)
            experts(1)

        @block.vector
        def _(dve):
            v = nc.vector
            count = [0]

            def link(ins):
                count[0] += 1
                ins.then_inc(chain, 1)
                dve.wait_ge(chain, count[0])

            def moments(src, col, done):
                for t in range(TB):
                    r = v.bn_stats(stats[:, col + t, :], src(t))
                link(r)
                for t in range(TB):
                    r = v.bn_aggr(mv[:, col + t, :], stats[:, col + t, :])
                link(r)
                cols = slice(col, col + TB)
                v.tensor_scalar(sq[:, cols], mv[:, cols, 1], EPS, None, ALU.add).then_inc(done, 1)

            def scale_and_shift(col, rooted, waited, done):
                dve.wait_ge(rooted, waited)
                cols = slice(col, col + TB)
                link(v.reciprocal(rstd[:, cols], root[:, cols]))
                v.scalar_tensor_tensor(out=shift[:, cols], in0=mv[:, cols, 0], scalar=-1.0, in1=rstd[:, cols],
                                       op0=ALU.mult, op1=ALU.mult).then_inc(done, 1)

            def route_moments(n, b):
                if n == 0:
                    dve.wait_ge(x_in[b], 16)
                moments(lambda t: res[:, b * TB + t, :], b * TB, r_var)

            def route_scale(n, b):
                scale_and_shift(b * TB, r_dev, n * BB + b + 1, r_s)

            def route_low(n, b):
                k, g0 = n % NB, n * BB + b
                tt = slice(b * TB, (b + 1) * TB)
                dve.wait_ge(r_hi, g0 + 1)
                v.tensor_tensor(x_s[:, k, tt, 1, :], xn[:, tt, :], x_s[:, k, tt, 0, :], ALU.subtract).then_inc(r_lo, 1)

            def choose(n):
                k = n % NB
                pri = prio[:, :].unsqueeze(1).to_broadcast((P, NT, E))
                dve.wait_ge(r_lg, (n + 1) * BB)
                link(v.tensor_tensor(lg[:, :, :], bank[4][:, 0:NT * E].rearrange("p (t e) -> p t e", e=E),
                                     b_r[:, :].unsqueeze(1).to_broadcast((P, NT, E)), ALU.add))
                for c in range(2):
                    link(v.tensor_reduce(top[:, c, :], lg[:, :, :], AX_X, ALU.max))
                    link(v.tensor_tensor(t0[:, :, :], lg[:, :, :], top[:, c, :].unsqueeze(2).to_broadcast((P, NT, E)), ALU.is_equal))
                    link(v.tensor_tensor(t1[:, :, :], t0[:, :, :], pri, ALU.mult))
                    link(v.tensor_reduce(pr[:, :], t1[:, :, :], AX_X, ALU.max))
                    link(v.tensor_tensor(oh[:, c, :, :], pri, pr[:, :].unsqueeze(2).to_broadcast((P, NT, E)), ALU.is_equal))
                    if c == 0:
                        link(v.scalar_tensor_tensor(out=lg[:, :, :], in0=oh[:, 0, :, :], scalar=FAR, in1=lg[:, :, :],
                                                    op0=ALU.mult, op1=ALU.add))
                v.tensor_tensor(mask16[:, :, :], oh[:, 0, :, :], oh[:, 1, :, :], ALU.add).then_inc(r_mask, 1)
                v.tensor_tensor(dlt[:, :], top[:, 1, :], top[:, 0, :], ALU.subtract).then_inc(r_dlt, 1)

            def weights(n):
                k = n % NB
                dve.wait_ge(r_ex, n + 1)
                link(v.tensor_scalar(den[:, :], ex[:, k, :], 1.0, None, ALU.add))
                link(v.reciprocal(den[:, :], den[:, :]))
                v.tensor_scalar(wgt[:, k, 0, :], den[:, :], 0.5, None, ALU.mult)
                link(v.scalar_tensor_tensor(out=wgt[:, k, 1, :], in0=den[:, :], scalar=0.5, in1=ex[:, k, :],
                                            op0=ALU.mult, op1=ALU.mult))

            def place(n):
                k = n % NB
                dve.wait_ge(r_pre, n + 1)
                link(v.tensor_scalar(cnt_i[:, :], bank[4][:, 256:256 + E], float(P - 1), None, ALU.add))
                link(v.tensor_scalar(til_i[:, :], cnt_i[:, :], 7, None, ALU.arith_shift_right))
                link(v.tensor_copy(til[:, :], til_i[:, :]))
                link(v.tensor_tensor(t2[:, :, :], before_e[:, :, :], til[:, :].unsqueeze(1).to_broadcast((P, E, E)), ALU.mult))
                link(v.tensor_reduce(start[:, :], t2[:, :, :], AX_X, ALU.add))
                link(v.scalar_tensor_tensor(out=base[:, :, :], in0=start[:, :].unsqueeze(1).to_broadcast((P, NT, E)), scalar=float(P),
                                            in1=bank[5][:, 0:NT * E].rearrange("p (t e) -> p t e", e=E),
                                            op0=ALU.mult, op1=ALU.add))
                for c, t in ((0, t0), (1, t1)):
                    link(v.tensor_tensor(t[:, :, :], oh[:, c, :, :], base[:, :, :], ALU.mult))
                    link(v.tensor_reduce(slot[:, :, c], t[:, :, :], AX_X, ALU.add))
                link(v.tensor_copy(slot_i[:, k, :, :], slot[:, :, :]))
                flat = slot_i[:, k, :, :].rearrange("p t c -> p (t c)")
                v.tensor_scalar(sp_i[:, 0, :], flat, 7, None, ALU.arith_shift_right)
                link(v.tensor_scalar(sp_i[:, 1, :], flat, P - 1, None, ALU.bitwise_and))
                link(v.tensor_copy(sp_f[:, :, :], sp_i[:, :, :]))
                I = 2 * NT
                if n:
                    dve.wait_ge(r_ids, n)
                for i in range(I):
                    r = v.tensor_scalar(pos_oh[:, i, :], iota16[:, :], sp_f[:, 1, i:i + 1], None, ALU.is_equal)
                r.then_inc(r_oh, 1)
                v.tensor_tensor(tile_oh[:, :, :], iota_tile[:, :].unsqueeze(1).to_broadcast((P, I, SLOT_TILES)),
                                     sp_f[:, 0, :].unsqueeze(2).to_broadcast((P, I, SLOT_TILES)), ALU.is_equal).then_inc(r_toh, 1)
                dve.wait_ge(r_toh, n + 1)
                v.tensor_tensor(tile_id[:, :, 0, :], tile_oh[:, :, :],
                                tok_id[:, :, :].rearrange("p t c -> p (t c)").unsqueeze(2).to_broadcast((P, I, SLOT_TILES)),
                                ALU.mult).then_inc(r_oh, 1)
                link(v.tensor_tensor(t3[:, :, :], iota_tile[:, :].unsqueeze(2).to_broadcast((P, SLOT_TILES, E)),
                                     start[:, :].unsqueeze(1).to_broadcast((P, SLOT_TILES, E)), ALU.is_ge))
                link(v.tensor_reduce(eid_f[:, :], t3[:, :, :], AX_X, ALU.add))
                v.tensor_scalar(eid[:, k, :], eid_f[:, :], -1.0, None, ALU.add).then_inc(r_eid, 1)
                dve.wait_ge(r_ids, n + 1)
                link(v.tensor_copy(ids_f[:, :], bank[5][:, 256:256 + SLOT_TILES]))
                link(v.scalar_tensor_tensor(out=dest_f[:, :], in0=bank[5][:, 256 + SLOT_TILES:256 + 2 * SLOT_TILES],
                                            scalar=float(BLOCK), in1=ids_f[:, :], op0=ALU.mult, op1=ALU.add))
                v.tensor_scalar(dest[:, k, :], dest_f[:, :], 2.0 * BLOCK, None, ALU.add)
                v.tensor_copy(ids[:, k, :], ids_f[:, :]).then_inc(r_idc, 1)

            def split_hidden(q):
                dve.wait_ge(f_hid, q + 1)
                if q >= 2:
                    dve.wait_ge(f_m2, q - 1)
                link(v.tensor_copy(h_s[:, q % 2, 0, :], hid[:, q % 2, :]))
                v.tensor_tensor(h_s[:, q % 2, 1, :], hid[:, q % 2, :], h_s[:, q % 2, 0, :], ALU.subtract).then_inc(f_hs, 1)

            def expert_out(q, e):
                dve.wait_ge(f_m2, q + 1)
                if q >= 2:
                    dve.wait_ge(f_y, q - 1)
                ps = bank[2 + q % 2]
                link(v.scalar_tensor_tensor(out=y_lo[:, q % 2, :], in0=ps[:, D:2 * D], scalar=1.0 / W_SCALE,
                                            in1=b_2[:, bass.ds(e, 1), :].rearrange("p a d -> p (a d)"),
                                            op0=ALU.mult, op1=ALU.add))
                if q >= NY:
                    dve.wait_ge(f_st[q % NY], 16 * (q // NY))
                v.scalar_tensor_tensor(out=y_sb[:, q % NY, :], in0=ps[:, 0:D], scalar=1.0 / W_SCALE, in1=y_lo[:, q % 2, :],
                                       op0=ALU.mult, op1=ALU.add).then_inc(f_y, 1)

            def experts(n):
                split_hidden(n * SLOT_TILES)
                for j in range(SLOT_TILES):
                    q = n * SLOT_TILES + j
                    if j + 1 < SLOT_TILES:
                        split_hidden(q + 1)
                    if j % LOAD == 0:
                        e_of = load_experts(mybir.EngineType.DVE, n, j)
                    expert_out(q, e_of[j % LOAD])

            def combine(n, b):
                k = n % NB
                dve.wait_ge(c_got[b], 16 * (n + 1))
                for c in range(2):
                    for t in range(TB):
                        i = b * TB + t
                        r = v.scalar_tensor_tensor(out=(part, res)[c][:, i, :], in0=back[:, b, c, t, :], scalar=wgt[:, k, c, i:i + 1],
                                                   in1=(res, part)[c][:, i, :], op0=ALU.mult, op1=ALU.add)
                    if c == 0:
                        link(r)
                r.then_inc(c_done, 1)
                dve.wait_ge(c_done, n * BB + b + 1)

            def attend_in(b):
                combine(0, b)
                moments(lambda t: res[:, b * TB + t, :], NT + b * TB, a_var)
                v.tensor_tensor(res_b[:, b, :, :], res[:, b * TB:(b + 1) * TB, :],
                                b_o[:, :].unsqueeze(1).to_broadcast((P, TB, D)), ALU.add).then_inc(a_rb, 1)

            def attend_scale(b):
                scale_and_shift(NT + b * TB, a_dev, b + 1, a_s)

            def attend_keys(b):
                dve.wait_ge(a_kvm, b + 1)
                if b >= 2:
                    dve.wait_ge(a_kk, b - 1)
                for h in range(2):
                    v.tensor_tensor(kv[:, b % 2, 2 * h:2 * h + 2, :], bank[1 + h][:, :].rearrange("p (t n) -> p t n", t=2),
                                    b_kv[:, :].unsqueeze(1).to_broadcast((P, 2, 2 * D)), ALU.add).then_inc(a_kv, 1)
                dve.wait_ge(a_kv, 2 * b + 2)
                v.tensor_tensor(kxv[:, b, :, :], kv[:, b % 2, :, 0:D], kv[:, b % 2, :, D:2 * D], ALU.mult).then_inc(a_kxv, 1)

            def attend_inverse(b):
                dve.wait_ge(a_rk, b + 1)
                col = 2 * NT + b * TB
                v.reciprocal(rstd[:, col:col + TB], root[:, col:col + TB]).then_inc(a_p, 1)

            def attend_sum(b):
                dve.wait_ge(a_rq, b + 1)
                col = 3 * NT + b * TB
                v.tensor_copy(kv_sum[:, b:b + 1], bank[3][:, 64:65]).then_inc(chain, 1)
                count[0] += 1
                v.reciprocal(rstd[:, col:col + TB], root[:, col:col + TB])
                dve.wait_ge(chain, count[0])
                v.tensor_scalar(wout_b[:, b, :], wout[:, :], kv_sum[:, b:b + 1], None, ALU.mult).then_inc(a_w, 1)
                dve.wait_ge(a_w, b + 1)

            def attend_out(b):
                col = 3 * NT + b * TB
                dve.wait_ge(a_rb, b + 1)
                dve.wait_ge(a_y, b + 1)
                for t in range(TB):
                    r = v.scalar_tensor_tensor(out=res[:, b * TB + t, :], in0=bank[5][:, t * D:(t + 1) * D],
                                               scalar=rstd[:, col + t:col + t + 1], in1=res_b[:, b, t, :], op0=ALU.mult, op1=ALU.add)
                r.then_inc(a_res, 1)
                dve.wait_ge(a_res, b + 1)
                route_moments(1, b)

            def split_w1(e):
                dve.wait_ge(w1_hi, e + 1)
                v.scalar_tensor_tensor(out=w1_s[:, e, 1, :], in0=w1_raw[:, e, :], scalar=W_SCALE,
                                       in1=w1_s[:, e, 0, :], op0=ALU.mult, op1=ALU.subtract).then_inc(w1_lo, 1)

            dve.wait_ge(consts, 14)
            dve.wait_ge(small_in, 32)
            for b in range(BB):
                route_moments(0, b)
            for b in range(BB):
                route_scale(0, b)
            for b in range(BB):
                route_low(0, b)
            choose(0)
            place(0)
            weights(0)
            for e in range(E):
                split_w1(e)
            dve.wait_ge(bias_in, 16 * 7)
            experts(0)

            slots([(attend_in, 0), (attend_sum, 3), (attend_keys, 2), (attend_scale, 0), (attend_out, 4),
                   (attend_inverse, 2), (lambda b: route_low(1, b), 5), (lambda b: route_scale(1, b), 4)])
            choose(1)
            place(1)
            weights(1)
            experts(1)
            for b in range(BB):
                combine(1, b)

        @block.tensor
        def _(pe):
            mm = nc.tensor.matmul

            def route_turn(n, b):
                g0 = n * BB + b
                pe.wait_ge(r_xn, g0 + 1)
                if g0:
                    pe.wait_ge(r_xT, g0)
                for t in range(TB):
                    r = nc.tensor.transpose(bank[7][:, t * P:(t + 1) * P], xn[:, b * TB + t, :], ident[:, :])
                r.then_inc(r_T, 1)

            def route_logits(n, b):
                pe.wait_ge(r_xT, n * BB + b + 1)
                for t in range(b * TB, (b + 1) * TB):
                    r = mm(bank[4][:, t * E:(t + 1) * E], xnT[:, t * P:(t + 1) * P], wr[:, :], start=True, stop=True)
                r.then_inc(r_lg, 1)

            def route_place(n):
                pe.wait_ge(r_mask, n + 1)
                m = mask16[:, :, :].rearrange("p t e -> p (t e)")
                mm(bank[5][:, 0:NT * E], before16[:, :], m, start=True, stop=False, skip_group_check=True)
                for s in range(1, NT):
                    mm(bank[5][:, s * E:NT * E], ones16[:, :], m[:, 0:(NT - s) * E], start=False, stop=(s == NT - 1), skip_group_check=True)
                for t in range(NT):
                    r = mm(bank[4][:, 256:256 + E], ones16[:, :], m[:, t * E:(t + 1) * E], start=(t == 0), stop=(t == NT - 1))
                r.then_inc(r_pre, 1)
                pe.wait_ge(r_oh, 3 * (n + 1))
                for i in range(2 * NT):
                    r = mm(bank[5][:, 256:256 + 2 * SLOT_TILES], pos_oh[:, i, :], tile_id[:, i, :, :].rearrange("p h s -> p (h s)"), start=(i == 0), stop=(i == 2 * NT - 1))
                r.then_inc(r_ids, 1)

            def tokens_T(q):
                pe.wait_ge(f_got[q % NG], 16 * (q // NG + 1))
                for h in range(2):
                    r = nc.tensor.transpose(bank16(4 + q % 2)[:, h * D:(h + 1) * D], got[:, q % NG, h * D:(h + 1) * D], ident16[:, :])
                r.then_inc(f_T, 1)

            def product1(q, e):
                pe.wait_ge(f_xT, q + 1)
                x_hi, x_lo = xT[:, q % 2, 0:D], xT[:, q % 2, D:2 * D]
                for c in range(CH):
                    o = bank[q % 2][:, c * P:(c + 1) * P]
                    w = [w1_s[:, bass.ds(e, 1), h, c * P:(c + 1) * P].rearrange("p a f -> p (a f)") for h in range(2)]
                    mm(o, w[0], x_hi, start=True, stop=False)
                    mm(o, w[0], x_lo, start=False, stop=False)
                    r = mm(o, w[1], x_hi, start=False, stop=True)
                r.then_inc(f_m1, 1)

            def product2(q, e):
                pe.wait_ge(f_hs, q + 1)
                o = bank[2 + q % 2]
                for c in range(CH):
                    w = w2_s[:, bass.ds(e, 1), c, :, :].rearrange("p a h d -> p (a h d)")
                    mm(o[:, 0:2 * D], h_s[:, q % 2, 0, c * P:(c + 1) * P], w, start=(c == 0), stop=False, skip_group_check=True)
                    r = mm(o[:, 0:D], h_s[:, q % 2, 1, c * P:(c + 1) * P], w[:, 0:D], start=False, stop=(c == CH - 1), skip_group_check=True)
                r.then_inc(f_m2, 1)

            def experts(n):
                q0, k = n * SLOT_TILES, n % NB
                pe.wait_ge(r_eid, n + 1)
                pe.wait_ge(r_idc, n + 1)
                tokens_T(q0)
                e_of = load_experts(mybir.EngineType.PE, n, 0)
                tokens_T(q0 + 1)
                product1(q0, e_of[0])
                e = e_of[0]
                for j in range(SLOT_TILES):
                    if j + 2 < SLOT_TILES:
                        tokens_T(q0 + j + 2)
                    if j + 1 < SLOT_TILES:
                        if (j + 1) % LOAD == 0:
                            after = load_experts(mybir.EngineType.PE, n, j + 1)
                        else:
                            after = e_of
                        product1(q0 + j + 1, after[(j + 1) % LOAD])
                    product2(q0 + j, e_of[j % LOAD])
                    e_of = after

            def attend_turn(b):
                pe.wait_ge(a_n, b + 1)
                for t in range(TB):
                    r = nc.tensor.transpose(bank[6][:, t * P:(t + 1) * P], a_xn[:, b, t, :], ident[:, :])
                r.then_inc(a_T, 1)

            def attend_project(b):
                pe.wait_ge(a_xTc, b + 1)
                if b:
                    pe.wait_ge(a_qe, 2 * b)
                    pe.wait_ge(a_kv, 2 * b)
                for t in range(TB):
                    r = mm(bank[1 + t // 2][:, (t % 2) * 2 * D:(t % 2 + 1) * 2 * D], a_xT[:, b, t * P:(t + 1) * P], wqkv[:, D:3 * D],
                           start=True, stop=True)
                r.then_inc(a_kvm, 1)
                mm(bank[0][:, :], wqkv[:, 0:D], a_xT[:, b, :], start=True, stop=True).then_inc(a_q, 1)

            def attend_sum(b):
                pe.wait_ge(a_qe, 2 * b + 2)
                for t in range(TB):
                    mm(bank[3][:, t:t + 1], q_sq[:, b, t * P:(t + 1) * P], ones[:, :], start=True, stop=True)
                pe.wait_ge(a_p, b + 1)
                col = 2 * NT + b * TB
                for t in range(TB):
                    r = mm(bank[3][:, 64:65], kxv[:, b, t, :], rstd[:, col + t:col + t + 1], start=(t == 0), stop=(t == TB - 1))
                r.then_inc(a_sum, 1)

            def attend_out(b):
                if b:
                    pe.wait_ge(a_res, b)
                pe.wait_ge(a_w, b + 1)
                for t in range(TB):
                    r = mm(bank[5][:, t * D:(t + 1) * D], q32[:, b, t * P:(t + 1) * P], wout_b[:, b, :], start=True, stop=True)
                r.then_inc(a_y, 1)

            def route_again(b):
                route_turn(1, b)
                route_logits(1, b)

            pe.wait_ge(consts, 14)
            pe.wait_ge(small_in, 32)
            for b in range(BB):
                route_turn(0, b)
                if b:
                    route_logits(0, b - 1)
            route_logits(0, BB - 1)
            pe.wait_ge(bias_in, 16 * 7)
            R = E * CH + 1
            nc.tensor.transpose(bank[5][:, 0:R], bias_rows[:, :], ident[0:R, 0:R]).then_inc(bias_T, 1)
            pe.wait_ge(bias_ok, 1)
            route_place(0)
            pe.wait_ge(w1_lo, E)
            pe.wait_ge(w2_lo, E)
            experts(0)
            pe.wait_ge(f_y, SLOT_TILES)
            slots([(attend_sum, 3), (attend_turn, 1), (attend_out, 3), (attend_project, 1), (route_again, 5)])
            route_place(1)
            experts(1)


_INS = ['L0_attn_x', 'L0_attn_Wqkv', 'L0_attn_bqkv', 'L0_attn_Wout', 'L0_attn_bout', 'L0_ffn_W_router',
        'L0_ffn_b_router', 'L0_ffn_W1', 'L0_ffn_b1', 'L0_ffn_W2', 'L0_ffn_b2']


def kernel(**inputs):
    import numpy as _np
    import concourse.bacc as _bacc
    from concourse import mybir as _mybir
    from concourse.bass_utils import run_bass_kernel_spmd as _run

    nc = _bacc.Bacc("TRN2", target_bir_lowering=False, num_devices=1)
    arrays, args = {}, []
    for name in _INS:
        a = _np.ascontiguousarray(inputs[name])
        arrays[f"in_{name}"] = a
        args.append(nc.dram_tensor(f"in_{name}", a.shape, _mybir.dt.from_np(a.dtype), kind="ExternalInput").ap())
    args.append(nc.dram_tensor("out_0", inputs['L0_attn_x'].shape, _mybir.dt.float32, kind="ExternalOutput").ap())
    macaron(nc, *args)
    r = _run(nc, [arrays], core_ids=[0])
    return r.results[0]["out_0"]
```
